# Optimizing a Trainium2 kernel written in Bass

```python
import numpy as np
import jax
import jax.numpy as jnp

def _softmax(x, axis=-1):
    return jax.nn.softmax(x, axis=axis)

def _gelu(x):
    return jax.nn.gelu(x, approximate=True)

def _silu(x):
    return jax.nn.silu(x)

def _sigmoid(x):
    return jax.nn.sigmoid(x)

def _layernorm(x, axis=-1, eps=1e-05):
    m = jnp.mean(x, axis=axis, keepdims=True)
    v = jnp.var(x, axis=axis, keepdims=True)
    return (x - m) / jnp.sqrt(v + eps)

def _scatter_add(tgt, idx, src, axis=0):
    return tgt.at[idx].add(src)

def _segment_sum(src, seg, n):
    return jax.ops.segment_sum(src, seg, n)
kernel_name = 'mk_sandwich_d2_jaxref_r8_f052e8'

def setup_inputs(seed: int=0):
    np.random.seed(seed)
    _w = jnp.asarray

    def _L0_attn_setup():
        import jax, jax.numpy as jnp
        import numpy as np
        EMBED_DIM = 256
        NUM_HEADS = 16
        HEAD_DIM = EMBED_DIM // NUM_HEADS
        BASE = 10000.0

        def rotate_half(x):
            half = x.shape[-1] // 2
            x1, x2 = (x[..., :half], x[..., half:])
            return jnp.concatenate([-x2, x1], axis=-1)

        def apply_rope(x, base=BASE):
            S, Dh = (x.shape[-2], x.shape[-1])
            inv_freq = 1.0 / base ** (jnp.arange(0, Dh, 2, dtype=jnp.float32) / Dh)
            t = jnp.arange(S, dtype=jnp.float32)
            freqs = jnp.einsum('i,j->ij', t, inv_freq)
            emb = jnp.concatenate([freqs, freqs], axis=-1)
            return x * jnp.cos(emb) + rotate_half(x) * jnp.sin(emb)
        key = jax.random.key(seed)
        ks = jax.random.split(key, 9)
        B, S, D = (2, 256, EMBED_DIM)
        xavier = lambda k, shape: jax.random.uniform(k, shape, jnp.float32, -1.0, 1.0) * float(np.sqrt(6.0 / (shape[0] + shape[1])))
        return {'x': jax.random.normal(ks[0], (B, S, D), jnp.float32), 'q_w': xavier(ks[1], (D, D)), 'k_w': xavier(ks[2], (D, D)), 'v_w': xavier(ks[3], (D, D)), 'q_b': jnp.zeros((D,), jnp.float32), 'k_b': jnp.zeros((D,), jnp.float32), 'v_b': jnp.zeros((D,), jnp.float32), 'out_w': xavier(ks[4], (D, D)), 'out_b': jnp.zeros((D,), jnp.float32)}
    _L0_attn_in = _L0_attn_setup()

    def _L0_ffn_setup():
        import jax, jax.numpy as jnp
        import numpy as np
        H = 256
        I = 176
        E = 16
        K = 2
        SI = I * 2

        def _swiglu(gu, inter):
            g, u = (gu[..., :inter], gu[..., inter:])
            return jax.nn.silu(g) * u
        key = jax.random.key(seed)
        ks = jax.random.split(key, 6)
        s = 0.02
        hidden_states = jax.random.normal(ks[0], (1, 128, H), dtype=jnp.float32)
        gate_w = jax.random.normal(ks[1], (E, H), dtype=jnp.float32) * s
        w_gate_up = jax.random.normal(ks[2], (E, H, 2 * I), dtype=jnp.float32) * s
        w_down = jax.random.normal(ks[3], (E, I, H), dtype=jnp.float32) * s
        shared_gate_up = jax.random.normal(ks[4], (H, 2 * SI), dtype=jnp.float32) * s
        shared_down = jax.random.normal(ks[5], (SI, H), dtype=jnp.float32) * s
        return {'hidden_states': hidden_states, 'gate_w': gate_w, 'w_gate_up': w_gate_up, 'w_down': w_down, 'shared_gate_up': shared_gate_up, 'shared_down': shared_down}
    _L0_ffn_in = _L0_ffn_setup()

    def _L1_attn_setup():
        import jax, jax.numpy as jnp
        import numpy as np
        B, T, D = (2, 256, 256)
        HK, HV, DK, DV = (16, 32, 128, 128)
        KEY_DIM = HK * DK
        VALUE_DIM = HV * DV
        CONV_DIM = 2 * KEY_DIM + VALUE_DIM
        KCONV = 4
        EPS = 1e-06

        def _l2norm(t):
            return t * jax.lax.rsqrt(jnp.sum(t * t, axis=-1, keepdims=True) + EPS)
        key = jax.random.key(seed)
        ks = jax.random.split(key, 10)
        s = 0.02
        return {'x': jax.random.normal(ks[0], (B, T, D), jnp.float32), 'w_qkv': jax.random.normal(ks[1], (D, CONV_DIM), jnp.float32) * s, 'w_z': jax.random.normal(ks[2], (D, VALUE_DIM), jnp.float32) * s, 'w_b': jax.random.normal(ks[3], (D, HV), jnp.float32) * s, 'w_a': jax.random.normal(ks[4], (D, HV), jnp.float32) * s, 'conv_w': jax.random.normal(ks[5], (KCONV, CONV_DIM), jnp.float32) * 0.25, 'dt_bias': jnp.ones((HV,), jnp.float32), 'A_log': jnp.log(jax.random.uniform(ks[6], (HV,), jnp.float32, 0.001, 16.0)), 'norm_w': jnp.ones((DV,), jnp.float32), 'w_out': jax.random.normal(ks[7], (VALUE_DIM, D), jnp.float32) * s}
    _L1_attn_in = _L1_attn_setup()

    def _L1_ffn_setup():
        import jax, jax.numpy as jnp
        import numpy as np
        ZERO_POINT = 128.0

        def _dequant(wq, scale):
            return (wq.astype(jnp.float32) - ZERO_POINT) * scale[:, None]
        key = jax.random.key(seed)
        ks = jax.random.split(key, 7)
        H, I = (256, 1024)
        B, S = (2, 256)
        hidden_state = jax.random.normal(ks[0], (B, S, H), dtype=jnp.float32)
        gate_w = jax.random.randint(ks[1], (I, H), 0, 32, dtype=jnp.int32)
        up_w = jax.random.randint(ks[2], (I, H), 0, 32, dtype=jnp.int32)
        down_w = jax.random.randint(ks[3], (H, I), 0, 32, dtype=jnp.int32)
        gate_scale = jax.random.uniform(ks[4], (I,), dtype=jnp.float32) * 0.02
        up_scale = jax.random.uniform(ks[5], (I,), dtype=jnp.float32) * 0.02
        down_scale = jax.random.uniform(ks[6], (H,), dtype=jnp.float32) * 0.02
        return {'hidden_state': hidden_state, 'gate_w': gate_w, 'gate_scale': gate_scale, 'up_w': up_w, 'up_scale': up_scale, 'down_w': down_w, 'down_scale': down_scale}
    _L1_ffn_in = _L1_ffn_setup()
    _d = {'L0_attn_x': _L0_attn_in['x'], 'L0_attn_q_w': _L0_attn_in['q_w'], 'L0_attn_k_w': _L0_attn_in['k_w'], 'L0_attn_v_w': _L0_attn_in['v_w'], 'L0_attn_q_b': _L0_attn_in['q_b'], 'L0_attn_k_b': _L0_attn_in['k_b'], 'L0_attn_v_b': _L0_attn_in['v_b'], 'L0_attn_out_w': _L0_attn_in['out_w'], 'L0_attn_out_b': _L0_attn_in['out_b'], 'L0_ffn_gate_w': _L0_ffn_in['gate_w'], 'L0_ffn_w_gate_up': _L0_ffn_in['w_gate_up'], 'L0_ffn_w_down': _L0_ffn_in['w_down'], 'L0_ffn_shared_gate_up': _L0_ffn_in['shared_gate_up'], 'L0_ffn_shared_down': _L0_ffn_in['shared_down'], 'L1_attn_w_qkv': _L1_attn_in['w_qkv'], 'L1_attn_w_z': _L1_attn_in['w_z'], 'L1_attn_w_b': _L1_attn_in['w_b'], 'L1_attn_w_a': _L1_attn_in['w_a'], 'L1_attn_conv_w': _L1_attn_in['conv_w'], 'L1_attn_dt_bias': _L1_attn_in['dt_bias'], 'L1_attn_A_log': _L1_attn_in['A_log'], 'L1_attn_norm_w': _L1_attn_in['norm_w'], 'L1_attn_w_out': _L1_attn_in['w_out'], 'L1_ffn_gate_w': _L1_ffn_in['gate_w'], 'L1_ffn_gate_scale': _L1_ffn_in['gate_scale'], 'L1_ffn_up_w': _L1_ffn_in['up_w'], 'L1_ffn_up_scale': _L1_ffn_in['up_scale'], 'L1_ffn_down_w': _L1_ffn_in['down_w'], 'L1_ffn_down_scale': _L1_ffn_in['down_scale']}
    _x0 = _d['L0_attn_x']
    _d['L0_attn_x'] = jax.random.normal(jax.random.fold_in(jax.random.key(seed), 1), (1, 2048, 256), dtype=_x0.dtype)
    del _x0
    return _d

def reference(L0_attn_x, L0_attn_q_w, L0_attn_k_w, L0_attn_v_w, L0_attn_q_b, L0_attn_k_b, L0_attn_v_b, L0_attn_out_w, L0_attn_out_b, L0_ffn_gate_w, L0_ffn_w_gate_up, L0_ffn_w_down, L0_ffn_shared_gate_up, L0_ffn_shared_down, L1_attn_w_qkv, L1_attn_w_z, L1_attn_w_b, L1_attn_w_a, L1_attn_conv_w, L1_attn_dt_bias, L1_attn_A_log, L1_attn_norm_w, L1_attn_w_out, L1_ffn_gate_w, L1_ffn_gate_scale, L1_ffn_up_w, L1_ffn_up_scale, L1_ffn_down_w, L1_ffn_down_scale):

    def _L0_attn_ref(x, q_w, k_w, v_w, q_b, k_b, v_b, out_w, out_b):
        import jax, jax.numpy as jnp
        import numpy as np
        EMBED_DIM = 256
        NUM_HEADS = 16
        HEAD_DIM = EMBED_DIM // NUM_HEADS
        BASE = 10000.0

        def rotate_half(x):
            half = x.shape[-1] // 2
            x1, x2 = (x[..., :half], x[..., half:])
            return jnp.concatenate([-x2, x1], axis=-1)

        def apply_rope(x, base=BASE):
            S, Dh = (x.shape[-2], x.shape[-1])
            inv_freq = 1.0 / base ** (jnp.arange(0, Dh, 2, dtype=jnp.float32) / Dh)
            t = jnp.arange(S, dtype=jnp.float32)
            freqs = jnp.einsum('i,j->ij', t, inv_freq)
            emb = jnp.concatenate([freqs, freqs], axis=-1)
            return x * jnp.cos(emb) + rotate_half(x) * jnp.sin(emb)
        B, S, D = x.shape
        H, Dh = (NUM_HEADS, HEAD_DIM)
        scaling = Dh ** (-0.5)
        q = (x @ q_w.T + q_b).reshape(B, S, H, Dh).transpose(0, 2, 1, 3)
        k = (x @ k_w.T + k_b).reshape(B, S, H, Dh).transpose(0, 2, 1, 3)
        v = (x @ v_w.T + v_b).reshape(B, S, H, Dh).transpose(0, 2, 1, 3)
        q = apply_rope(q)
        k = apply_rope(k)
        attn = jnp.einsum('bhqd,bhkd->bhqk', q, k) * scaling
        probs = jax.nn.softmax(attn, axis=-1)
        out = jnp.einsum('bhqk,bhkd->bhqd', probs, v)
        out = out.transpose(0, 2, 1, 3).reshape(B, S, D)
        return out @ out_w.T + out_b

    def _L0_ffn_ref(hidden_states, gate_w, w_gate_up, w_down, shared_gate_up, shared_down):
        import jax, jax.numpy as jnp
        import numpy as np
        H = 256
        I = 176
        E = 16
        K = 2
        SI = I * 2

        def _swiglu(gu, inter):
            g, u = (gu[..., :inter], gu[..., inter:])
            return jax.nn.silu(g) * u
        orig_shape = hidden_states.shape
        x = hidden_states.reshape(-1, H)
        logits = jnp.einsum('th,eh->te', x, gate_w)
        scores = jax.nn.softmax(logits, axis=-1)
        topk_w, topk_idx = jax.lax.top_k(scores, K)
        combine = jnp.sum(jax.nn.one_hot(topk_idx, E, dtype=x.dtype) * topk_w[..., None], axis=1)
        gu = jnp.einsum('th,ehj->etj', x, w_gate_up)
        h = _swiglu(gu, I)
        y = jnp.einsum('eti,eih,te->th', h, w_down, combine)
        gu_s = x @ shared_gate_up
        y = y + _swiglu(gu_s, SI) @ shared_down
        return y.reshape(orig_shape)

    def _L1_attn_ref(x, w_qkv, w_z, w_b, w_a, conv_w, dt_bias, A_log, norm_w, w_out):
        import jax, jax.numpy as jnp
        import numpy as np
        B, T, D = (2, 256, 256)
        HK, HV, DK, DV = (16, 32, 128, 128)
        KEY_DIM = HK * DK
        VALUE_DIM = HV * DV
        CONV_DIM = 2 * KEY_DIM + VALUE_DIM
        KCONV = 4
        EPS = 1e-06

        def _l2norm(t):
            return t * jax.lax.rsqrt(jnp.sum(t * t, axis=-1, keepdims=True) + EPS)
        Bx, Tx, _ = x.shape
        mixed = x @ w_qkv
        z = x @ w_z
        b_raw = x @ w_b
        a_raw = x @ w_a
        Kc = conv_w.shape[0]
        xp = jnp.pad(mixed, ((0, 0), (Kc - 1, 0), (0, 0)))
        windows = jnp.stack([xp[:, k:k + Tx, :] for k in range(Kc)], axis=2)
        mixed = jax.nn.silu(jnp.sum(windows * conv_w[None, None], axis=2))
        q, k, v = jnp.split(mixed, [KEY_DIM, 2 * KEY_DIM], axis=-1)
        q = q.reshape(Bx, Tx, HK, DK)
        k = k.reshape(Bx, Tx, HK, DK)
        v = v.reshape(Bx, Tx, HV, DV)
        rep = HV // HK
        if rep > 1:
            q = jnp.repeat(q, rep, axis=2)
            k = jnp.repeat(k, rep, axis=2)
        beta = jax.nn.sigmoid(b_raw)
        g = -(jnp.exp(A_log) * jax.nn.softplus(a_raw + dt_bias))
        q = _l2norm(q) * DK ** (-0.5)
        k = _l2norm(k)
        state0 = jnp.zeros((Bx, HV, DK, DV), x.dtype)

        def step(state, inp):
            q_t, k_t, v_t, g_t, b_t = inp
            state = state * jnp.exp(g_t)[:, :, None, None]
            kv_mem = jnp.einsum('bhd,bhde->bhe', k_t, state)
            delta = (v_t - kv_mem) * b_t[:, :, None]
            state = state + jnp.einsum('bhd,bhe->bhde', k_t, delta)
            out_t = jnp.einsum('bhd,bhde->bhe', q_t, state)
            return (state, out_t)
        mv = lambda t: jnp.moveaxis(t, 1, 0)
        _, outs = jax.lax.scan(step, state0, (mv(q), mv(k), mv(v), mv(g), mv(beta)))
        core = jnp.moveaxis(outs, 0, 1)
        z_heads = z.reshape(Bx, Tx, HV, DV)
        rms_inv = jax.lax.rsqrt(jnp.mean(core * core, axis=-1, keepdims=True) + EPS)
        core = norm_w * (core * rms_inv) * jax.nn.silu(z_heads)
        return core.reshape(Bx, Tx, VALUE_DIM) @ w_out

    def _L1_ffn_ref(hidden_state, gate_w, gate_scale, up_w, up_scale, down_w, down_scale):
        import jax, jax.numpy as jnp
        import numpy as np
        ZERO_POINT = 128.0

        def _dequant(wq, scale):
            return (wq.astype(jnp.float32) - ZERO_POINT) * scale[:, None]
        Wg = _dequant(gate_w, gate_scale)
        Wu = _dequant(up_w, up_scale)
        Wd = _dequant(down_w, down_scale)
        g = jnp.einsum('bsh,ih->bsi', hidden_state, Wg)
        u = jnp.einsum('bsh,ih->bsi', hidden_state, Wu)
        h = jax.nn.silu(g) * u
        return jnp.einsum('bsi,hi->bsh', h, Wd)
    x = L0_attn_x
    x = x + _layernorm(_L0_attn_ref(_layernorm(x, axis=-1), L0_attn_q_w, L0_attn_k_w, L0_attn_v_w, L0_attn_q_b, L0_attn_k_b, L0_attn_v_b, L0_attn_out_w, L0_attn_out_b), axis=-1)
    x = x + _layernorm(_L0_ffn_ref(_layernorm(x, axis=-1), L0_ffn_gate_w, L0_ffn_w_gate_up, L0_ffn_w_down, L0_ffn_shared_gate_up, L0_ffn_shared_down), axis=-1)
    x = x + _layernorm(_L1_attn_ref(_layernorm(x, axis=-1), L1_attn_w_qkv, L1_attn_w_z, L1_attn_w_b, L1_attn_w_a, L1_attn_conv_w, L1_attn_dt_bias, L1_attn_A_log, L1_attn_norm_w, L1_attn_w_out), axis=-1)
    x = x + _layernorm(_L1_ffn_ref(_layernorm(x, axis=-1), L1_ffn_gate_w, L1_ffn_gate_scale, L1_ffn_up_w, L1_ffn_up_scale, L1_ffn_down_w, L1_ffn_down_scale), axis=-1)
    return x

_drawn_inputs = setup_inputs


def setup_inputs(seed=0):
    import zlib

    import numpy as np

    out = dict(_drawn_inputs(seed))
    spreads = {'L0_attn_q_b': (0.0, 0.1),
     'L0_attn_k_b': (0.0, 0.1),
     'L0_attn_v_b': (0.0, 0.1),
     'L0_attn_out_b': (0.0, 0.1),
     'L1_attn_dt_bias': (1.0, 0.6),
     'L1_attn_norm_w': (1.0, 0.2)}
    factors = {'L1_attn_w_a': 3.543}
    for name, (base, spread) in spreads.items():
        noise = np.random.default_rng([zlib.crc32(name.encode()), seed]).standard_normal(out[name].shape)
        drawn = base * np.exp(spread * noise) if base else spread * noise
        out[name] = jnp.asarray(drawn.astype(out[name].dtype))
    for name, factor in factors.items():
        out[name] = (out[name] * factor).astype(out[name].dtype)
    return out
```

```python
from contextlib import ExitStack

import concourse.bass as bass
from concourse import mybir

F32 = mybir.dt.float32
BF16 = mybir.dt.bfloat16
U32 = mybir.dt.uint32
I32 = mybir.dt.int32
ALU = mybir.AluOpType
ACT = mybir.ActivationFunctionType
AX = mybir.AxisListType
ds = bass.ds

P = 128
T = 2048
D = 256
NT = T // P
KD = D // P
LN_EPS = 1e-5

HEADS, DH = 16, 16
PARTS = 6
SPLIT_ROWS = PARTS * DH
MAX_ROWS = 3
SCORE_ROWS = SPLIT_ROWS + MAX_ROWS

EXPERTS, INTER = 16, 176
SHARED_PARTS = 2
ALL_EXPERTS = EXPERTS + SHARED_PARTS
HCAT = ALL_EXPERTS * INTER
HT = -(-HCAT // P)

FFN = 1024
FT = FFN // P


def flat(ap):
    names = "abcde"[: len(ap.shape) - 1]
    return ap.rearrange(f"p {' '.join(names)} -> p ({' '.join(names)})")


class Core:

    def __init__(self, nc, ctx):
        self.nc, self.ctx, self.n = nc, ctx, 0
        self.X = self.sb(ctx, "residual", [P, NT, D], F32)
        self.XT = self.sb(ctx, "normed_t", [P, KD, T], F32)
        self.Y = self.sb(ctx, "branch", [P, NT, D], F32)
        self.ident = self.sb(ctx, "ident", [P, P], F32)
        self.identb = self.sb(ctx, "identb", [P, P], BF16)
        self.ones = self.sb(ctx, "ones_row", [1, P], F32)

    def sb(self, ctx, name, shape, dt):
        return ctx.enter_context(self.nc.sbuf_tensor(name, shape, dt))

    def ps(self, ctx, name, shape, dt=F32):
        return ctx.enter_context(self.nc.psum_tensor(name, shape, dt))

    def sem(self, ctx, name):
        return ctx.enter_context(self.nc.semaphore(name))


def setup(c, x_dram):
    nc = c.nc
    with ExitStack() as ctx:
        x_in = c.sem(ctx, "x_in")
        ident0 = c.sem(ctx, "ident_zeroed")
        ident1 = c.sem(ctx, "ident_made")
        block = ctx.enter_context(nc.Block())

        @block.sync
        def _(sp):
            sp.dma_start(c.X[:, :, :], x_dram.rearrange("(t p) d -> p t d", p=P)).then_inc(x_in, 16)
            sp.wait_ge(x_in, 16)

        @block.gpsimd
        def _(pool):
            pool.memset(c.ident[:, :], 0.0).then_inc(ident0, 1)
            pool.memset(c.ones[:, :], 1.0)
            pool.wait_ge(ident0, 1)
            pool.affine_select(out=c.ident[:, :], in_=c.ident[:, :], compare_op=ALU.not_equal, fill=1.0,
                               base=0, pattern=[[-1, P]], channel_multiplier=1).then_inc(ident1, 1)
            pool.wait_ge(ident1, 1)
            pool.tensor_copy(c.identb[:, :], c.ident[:, :])


def norm_phase(c, tag, add_branch, want_t=True, out_dram=None):
    nc = c.nc
    rounds = (1 if add_branch else 0) + (1 if want_t else 0)
    with ExitStack() as ctx:
        normed = c.sb(ctx, f"{tag}_normed", [P, NT, D], F32)
        stats = c.sb(ctx, f"{tag}_stats", [P, NT, 6], F32)
        mv = c.sb(ctx, f"{tag}_mean_var", [P, NT, 2], F32)
        rstd = c.sb(ctx, f"{tag}_rstd", [P, NT], F32)
        mhalf = c.sb(ctx, f"{tag}_minus_half", [P, NT], F32)
        tp = [c.ps(ctx, f"{tag}_tp{i}", [P, 2, KD, P]) for i in range(2)]
        stats_done = c.sem(ctx, f"{tag}_stats_done")
        aggr_done = c.sem(ctx, f"{tag}_aggr_done")
        var_done = c.sem(ctx, f"{tag}_var_done")
        rstd_done = c.sem(ctx, f"{tag}_rstd_done")
        scaled = c.sem(ctx, f"{tag}_scaled")
        added = c.sem(ctx, f"{tag}_added") if add_branch else None
        turned = c.sem(ctx, f"{tag}_turned") if want_t else None
        copied = c.sem(ctx, f"{tag}_copied") if want_t else None
        stored = c.sem(ctx, f"{tag}_stored") if out_dram is not None else None
        block = ctx.enter_context(nc.Block())

        @block.vector
        def _(dve):
            def normalise(src, r):
                with dve.Fori(0, NT) as t:
                    dve.bn_stats(stats[:, ds(t, 1), :].rearrange("p a s -> p (a s)"),
                                 src[:, ds(t, 1), :].rearrange("p a s -> p (a s)")).then_inc(stats_done, 1)
                dve.wait_ge(stats_done, NT * (r + 1))
                for t in range(NT):
                    last = dve.bn_aggr(mv[:, t, :], stats[:, t, :])
                last.then_inc(aggr_done, 1)
                dve.wait_ge(rstd_done, 2 * (r + 1))
                with dve.Fori(0, NT) as t:
                    dve.tensor_scalar(normed[:, ds(t, 1), :].rearrange("p a s -> p (a s)"),
                                      src[:, ds(t, 1), :].rearrange("p a s -> p (a s)"),
                                      mv[:, ds(t, 1), 0:1].rearrange("p a s -> p (a s)"), rstd[:, ds(t, 1)],
                                      ALU.subtract, ALU.mult).then_inc(scaled, 1)

            if add_branch:
                normalise(c.Y, 0)
                dve.wait_ge(scaled, NT)
                dve.tensor_tensor(flat(c.X[:, :, :]), flat(c.X[:, :, :]), flat(normed[:, :, :]),
                                  ALU.add).then_inc(added, 1)
                dve.wait_ge(added, 1)
            if want_t:
                normalise(c.X, rounds - 1)

        @block.gpsimd
        def _(pool):
            pool.memset(mhalf[:, :], -0.5).then_inc(var_done, 1)
            for r in range(rounds):
                pool.wait_ge(aggr_done, r + 1)
                pool.tensor_scalar(rstd[:, :], mv[:, :, 1], LN_EPS, None, ALU.add).then_inc(rstd_done, 1)
                pool.wait_ge(rstd_done, 2 * r + 1)
                pool.wait_ge(var_done, 1)
                pool.tensor_tensor(rstd[:, :], rstd[:, :], mhalf[:, :], ALU.pow).then_inc(rstd_done, 1)

        if want_t:
            transpose_tiles(c, block, normed, c.XT, tp, scaled, NT * (rounds - 1), turned, copied)

        if out_dram is not None:
            @block.sync
            def _(sp):
                sp.wait_ge(added, 1)
                sp.dma_start(out_dram.rearrange("(t p) d -> p t d", p=P), c.X[:, :, :]).then_inc(stored, 16)
                sp.wait_ge(stored, 16)


def transpose_tiles(c, block, src, dst, tp, ready, ready_base, turned, copied):

    @block.tensor
    def _(pe):
        for i in range(NT // 2):
            if ready is not None:
                pe.wait_ge(ready, ready_base + 2 * i + 2)
            if i >= 2:
                pe.wait_ge(copied, i - 1)
            for j in range(2):
                for k in range(KD):
                    last = pe.transpose(tp[i % 2][:, j, k, :], src[:, 2 * i + j, k * P:(k + 1) * P],
                                        c.ident[:, :])
            last.then_inc(turned, 1)

    @block.scalar
    def _(act):
        for i in range(NT // 2):
            act.wait_ge(turned, i + 1)
            out = dst[:, :, 2 * i * P:(2 * i + 2) * P].rearrange("p k (j c) -> p j k c", j=2)
            act.activation(out, tp[i % 2][:, :, :, :], ACT.Copy).then_inc(copied, 1)


def qkv_phase(c, QT, KT, V, w_dram, bias_dram, rope_dram):
    nc = c.nc
    with ExitStack() as ctx:
        W = flat(c.Y[:, 0:6, :]).rearrange("p (k n) -> p k n", k=KD)
        bias = c.sb(ctx, "qkv_bias", [1, 3 * D], F32)
        rope = c.sb(ctx, "rope", [P, NT, 2, DH], F32)
        xs = [c.Y[:, 6 + j, :].rearrange("p (k n) -> p k n", k=KD) for j in range(2)]
        QK = 2 * HEADS
        cosp = flat(c.Y[:, 8:10, :]).rearrange("p (h d) -> p h d", h=QK)
        rot = flat(c.Y[:, 10:12, :]).rearrange("p (h d) -> p h d", h=QK)
        rest = flat(c.Y[:, 12:14, :]).rearrange("p (h d) -> p h d", h=QK)
        hi, mid = (c.Y[:, 14 + j, :].bitcast(BF16).rearrange("p (h d) -> p h d", h=QK) for j in range(2))
        lo = c.sb(ctx, "lo", [P, QK, DH], BF16)
        stack = [c.sb(ctx, f"stack{i}", [P, HEADS, PARTS, DH], BF16) for i in range(2)]
        qk_ps = [c.ps(ctx, f"qk_ps{j}", [P, QK, DH]) for j in range(2)]
        v_ps = [c.ps(ctx, f"v_ps{j}", [P, 512]) for j in range(2)]
        tp = [c.ps(ctx, f"stack_tp{i}", [P, 8, P], BF16) for i in range(4)]
        loaded = c.sem(ctx, "qkv_loaded")
        xs_free = c.sem(ctx, "xs_free")
        xs_ready = c.sem(ctx, "xs_ready")
        qkv_free = c.sem(ctx, "qkv_free")
        qkv_done = c.sem(ctx, "qkv_done")
        rope_step = c.sem(ctx, "rope_step")
        hi_done = c.sem(ctx, "hi_done")
        rest_done = c.sem(ctx, "rest_done")
        mid_done = c.sem(ctx, "mid_done")
        lo_done = c.sem(ctx, "lo_done")
        q_stacked = c.sem(ctx, "q_stacked")
        k_stacked = c.sem(ctx, "k_stacked")
        tp_done = c.sem(ctx, "stack_tp_done")
        tp_copied = c.sem(ctx, "stack_tp_copied")
        block = ctx.enter_context(nc.Block())

        @block.sync
        def _(sp):
            sp.dma_start(W, w_dram).then_inc(loaded, 16)
            sp.dma_start(bias[:, :], bias_dram).then_inc(loaded, 16)
            sp.dma_start(rope[:, :, :, :], rope_dram).then_inc(loaded, 16)

        @block.gpsimd
        def _(pool):
            with pool.Fori(0, NT // 2) as i:
                for j in range(2):
                    t = 2 * i + j
                    pool.wait_ge(xs_free, t + 1)
                    pool.tensor_copy(xs[j], c.XT[:, :, ds(t * P, P)]).then_inc(xs_ready, 1)

        @block.tensor
        def _(pe):
            pe.sem_inc(xs_free, 2)
            pe.sem_inc(tp_done, 4)
            pe.wait_ge(loaded, 48)
            with pe.Fori(0, NT // 2) as i:
                for j in range(2):
                    t = 2 * i + j
                    pe.wait_ge(xs_ready, t + 1)
                    pe.wait_ge(qkv_free, t + 1)
                    for out, lo_, n in ((flat(qk_ps[j][:, :, :]), 0, 2 * D), (v_ps[j][:, 0:D], 2 * D, D)):
                        for k in range(KD):
                            pe.matmul(out, xs[j][:, k, :], W[:, k, lo_:lo_ + n], start=(k == 0), stop=False)
                        last = pe.matmul(out, c.ones[:, :], bias[:, lo_:lo_ + n], start=False, stop=True)
                    last.then_inc(qkv_done, 1)
                    for s, stacked in ((0, q_stacked), (1, k_stacked)):
                        pe.wait_ge(stacked, t + 1)
                        for half in range(2):
                            pe.wait_ge(tp_copied, 4 * t + 2 * s + half + 1)
                            for h in range(8):
                                last = pe.transpose(tp[2 * s + half][0:SPLIT_ROWS, h, :],
                                                    stack[s][:, 8 * half + h, :, :].rearrange("p a b -> p (a b)"),
                                                    c.identb[:, :])
                            last.then_inc(tp_done, 1)

        @block.scalar
        def _(act):
            act.sem_inc(tp_copied, 4)
            with act.Fori(0, NT // 2) as i:
                for j in range(2):
                    t = 2 * i + j
                    act.wait_ge(qkv_done, t + 1)
                    act.activation(V[:, ds(t, 1), :, :].rearrange("p a h d -> p (a h d)"), v_ps[j][:, 0:D],
                                   ACT.Copy).then_inc(xs_free, 1)
                    act.wait_ge(rest_done, 2 * t + 1)
                    act.activation(flat(hi), flat(rest), ACT.Copy).then_inc(hi_done, 1)
                    act.wait_ge(rest_done, 2 * t + 2)
                    act.activation(flat(mid), flat(rest), ACT.Copy).then_inc(mid_done, 1)
                    act.wait_ge(lo_done, t + 1)
                    act.wait_ge(tp_done, 4 * t + 4)
                    for part, src in ((0, hi), (3, hi), (5, hi), (1, mid), (4, mid), (2, lo)):
                        last = act.activation(stack[1][:, :, part, :], src[:, HEADS:QK, :], ACT.Copy)
                    last.then_inc(k_stacked, 1)
                    for s, dst in ((0, QT), (1, KT)):
                        for half in range(2):
                            act.wait_ge(tp_done, 4 * t + 2 * s + half + 1 + 4)
                            act.activation(dst[0:SPLIT_ROWS, 8 * half:8 * half + 8, ds(t * P, P)],
                                           tp[2 * s + half][0:SPLIT_ROWS, :, :], ACT.Copy).then_inc(tp_copied, 1)

        @block.vector
        def _(dve):
            dve.sem_inc(qkv_free, 2)
            half = DH // 2
            dve.memset(KT[SPLIT_ROWS:SCORE_ROWS, :, :], 1.0)
            dve.wait_ge(loaded, 48)
            with dve.Fori(0, NT // 2) as i:
                for j in range(2):
                    t = 2 * i + j
                    src = qk_ps[j]

                    def table(k, a, n):
                        return rope[:, ds(t, 1), k, a:a + n].broadcast_to([P, QK, n])

                    dve.wait_ge(qkv_done, t + 1)
                    dve.tensor_tensor(cosp, src[:, :, :], table(0, 0, DH), ALU.mult)
                    dve.tensor_tensor(rot[:, :, 0:half], src[:, :, half:DH], table(1, 0, half), ALU.mult)
                    dve.tensor_tensor(rot[:, :, half:DH], src[:, :, 0:half], table(1, half, half),
                                      ALU.mult).then_inc(qkv_free, 1)
                    dve.wait_ge(qkv_free, t + 3)
                    dve.tensor_tensor(rest, cosp, rot, ALU.add).then_inc(rest_done, 1)
                    dve.wait_ge(hi_done, t + 1)
                    dve.tensor_tensor(rest, rest, hi, ALU.subtract).then_inc(rest_done, 1)
                    dve.wait_ge(mid_done, t + 1)
                    dve.tensor_tensor(lo[:, :, :], rest, mid, ALU.subtract).then_inc(lo_done, 1)
                    dve.wait_ge(lo_done, t + 1)
                    dve.wait_ge(tp_done, 4 * t + 2)
                    for part, s in ((0, hi), (1, hi), (2, hi), (3, mid), (4, mid), (5, lo)):
                        last = dve.tensor_copy(stack[0][:, :, part, :], s[:, 0:HEADS, :])
                    last.then_inc(q_stacked, 1)
                    dve.wait_ge(k_stacked, t + 1)


def attention_phase(c, QT, KT, V):
    nc = c.nc
    QB = 4
    BQ = T // QB
    with ExitStack() as ctx:
        probs = c.XT
        vs = c.sb(ctx, "v_staged", [P, NT, 32], F32)
        part_max = c.sb(ctx, "part_max", [P, NT, 4], F32)
        neg_max = c.sb(ctx, "neg_max", [P, NT], F32)
        max_parts = c.sb(ctx, "max_parts", [P, MAX_ROWS + 2, NT], BF16)
        PAD = (MAX_ROWS + 2) * NT
        max_t = c.sb(ctx, "max_t", [MAX_ROWS * NT, P], BF16)
        out_sb = c.sb(ctx, "out_sb", [P, BQ], F32)
        rden = c.sb(ctx, "rden", [P, NT], F32)
        mx = [c.ps(ctx, f"mx{i}", [P, 512]) for i in range(2)]
        sc = [c.ps(ctx, f"sc{i}", [P, 2, 512]) for i in range(2)]
        o_ps = c.ps(ctx, "o_ps", [P, 512])
        tr_ps = c.ps(ctx, "tr_ps", [P, 512])
        s = {n: c.sem(ctx, n) for n in (
            "pad_set", "v_staged_sem", "mx_done", "mx_free", "sc_done", "exp_done", "pv_done", "max_step",
            "parts_ready", "max_turned", "max_copied", "rows_in", "o_copied", "o_turned", "rden_done", "o_free")}
        block = ctx.enter_context(nc.Block())

        def program(engine, emit):
            with engine.Fori(0, 2) as i:
                emit(i, True, False)
            with engine.Fori(2, HEADS) as i:
                emit(i, True, True)
            with engine.Fori(HEADS, HEADS + 2) as i:
                emit(i, False, True)

        @block.gpsimd
        def _(pool):
            pool.memset(vs[:, :, DH:32], 0.0).then_inc(s["pad_set"], 1)
            pool.wait_ge(s["pad_set"], 1)
            pool.memset(vs[:, :, DH:DH + 1], 1.0).then_inc(s["pad_set"], 1)
            pool.wait_ge(s["pad_set"], 2)

            with pool.Fori(0, HEADS) as h:
                for kt in range(NT):
                    pool.wait_ge(s["pv_done"], NT * h + kt + 1)
                    pool.tensor_copy(vs[:, kt, 0:DH], V[:, kt, ds(h, 1), :].rearrange("p a d -> p (a d)")
                                     ).then_inc(s["v_staged_sem"], 1)

        @block.tensor
        def _(pe):
            pe.sem_inc(s["mx_free"], 2)
            pe.sem_inc(s["pv_done"], NT)
            pe.sem_inc(s["max_turned"], 1)

            def emit(i, do_max, do_exp):
                h = i - 2

                def q_cols(head, a, n, rows=SCORE_ROWS):
                    return QT[0:rows, ds(head, 1), a:a + n].rearrange("p a b -> p (a b)")

                def k_cols(head, a, n, rows=SCORE_ROWS):
                    return KT[0:rows, ds(head, 1), a:a + n].rearrange("p a b -> p (a b)")

                def scores(kt, u):
                    pe.wait_ge(s["exp_done"], 2 * NT * h + 2 * kt + u + 1)
                    for b in range(2):
                        last = pe.matmul(sc[u][:, b, :], k_cols(h, kt * P, P), q_cols(h, (2 * u + b) * BQ, BQ),
                                         start=True, stop=True)
                    last.then_inc(s["sc_done"], 1)

                def maxima(qt, u):
                    for b in (2 * u, 2 * u + 1):
                        pe.wait_ge(s["mx_free"], 4 * NT * i + 4 * qt + b + 1)
                        pe.matmul(mx[b % 2][:, :], q_cols(i, qt * P, P, SPLIT_ROWS),
                                  k_cols(i, b * 512, 512, SPLIT_ROWS), start=True, stop=True
                                  ).then_inc(s["mx_done"], 1)

                def weigh(kt):
                    pe.wait_ge(s["exp_done"], 2 * NT * h + 2 * kt + 2 + 2)
                    pe.wait_ge(s["v_staged_sem"], NT * h + kt + 1)
                    if kt == 0:
                        pe.wait_ge(s["o_free"], h + 1)
                    for qb in range(QB):
                        last = pe.matmul(o_ps[32 * qb:32 * qb + 32, :], vs[:, kt, :],
                                         probs[:, kt % 2, qb * BQ:(qb + 1) * BQ], start=(kt == 0),
                                         stop=(kt == NT - 1))
                    last.then_inc(s["pv_done"], 1)

                if do_exp:
                    pe.wait_ge(s["rows_in"], 16 * MAX_ROWS * (h + 2))
                for kt in range(NT):
                    for u in range(2):
                        if do_exp:
                            scores(kt, u)
                        if do_max:
                            maxima(kt, u)
                    if do_exp and kt:
                        weigh(kt - 1)
                if do_exp:
                    weigh(NT - 1)
                if do_max:
                    pe.wait_ge(s["max_copied"], i + 1)
                    pe.wait_ge(s["parts_ready"], i + 1)
                    pe.transpose(tr_ps[0:PAD, 0:P // 2].bitcast(BF16),
                                 max_parts[:, :, :].rearrange("p a b -> p (a b)"), c.identb[:, :]
                                 ).then_inc(s["max_turned"], 1)
                if do_exp:
                    pe.wait_ge(s["o_copied"], h + 1)
                    for j in range(QB):
                        last = pe.transpose(o_ps[:, j * P:(j + 1) * P], out_sb[:, j * P:(j + 1) * P],
                                            c.ident[:, :])
                    last.then_inc(s["o_turned"], 1)

            program(pe, emit)

        @block.scalar
        def _(act):
            act.sem_inc(s["exp_done"], 2)
            act.sem_inc(s["max_copied"], 1)

            def emit(i, do_max, do_exp):
                h = i - 2
                if do_exp:
                    for kt in range(NT):
                        for u in range(2):
                            act.wait_ge(s["sc_done"], 2 * NT * h + 2 * kt + u + 1)
                            if u == 0:
                                act.wait_ge(s["pv_done"], NT * h + kt + NT - 1)
                            act.activation(probs[:, kt % 2, u * 2 * BQ:(u + 1) * 2 * BQ], flat(sc[u][:, :, :]),
                                           ACT.Exp, scale=float(DH) ** -0.5).then_inc(s["exp_done"], 1)
                    act.wait_ge(s["pv_done"], NT * h + NT + NT)
                    act.activation(out_sb[:, :], o_ps[:, :], ACT.Copy).then_inc(s["o_copied"], 1)
                if do_max:
                    act.wait_ge(s["max_turned"], i + 2)
                    act.wait_ge(s["rows_in"], 16 * MAX_ROWS * (i + 1))
                    act.activation(max_t[:, :], tr_ps[0:MAX_ROWS * NT, 0:P // 2].bitcast(BF16), ACT.Copy
                                   ).then_inc(s["max_copied"], 1)

            program(act, emit)

        @block.sync
        def _(sp):
            sp.sem_inc(s["rows_in"], 16 * MAX_ROWS)
            with sp.Fori(0, HEADS) as h:
                sp.wait_ge(s["max_copied"], h + 2)
                for part in range(MAX_ROWS):
                    row = SPLIT_ROWS + part
                    dst = QT[row:row + 1, ds(h, 1), :].rearrange("r a (t c) -> r (a t) c", t=NT)
                    sp.dma_start(dst, max_t[part * NT:(part + 1) * NT, :]).then_inc(s["rows_in"], 16)

        @block.vector
        def _(dve):
            dve.sem_inc(s["o_free"], 1)
            dve.memset(max_parts[:, MAX_ROWS:, :], 0.0)

            def emit(i, do_max, do_exp):
                h = i - 2
                links = 2 * MAX_ROWS - 1

                def chained(ins, n):
                    ins.then_inc(s["max_step"], 1)
                    dve.wait_ge(s["max_step"], links * i + n)

                if do_max:
                    for qt in range(NT):
                        for b in range(4):
                            dve.wait_ge(s["mx_done"], 4 * NT * i + 4 * qt + b + 1)
                            dve.reduce_max(part_max[:, qt, b:b + 1], mx[b % 2][:, :], AX.X
                                           ).then_inc(s["mx_free"], 1)
                    dve.wait_ge(s["mx_free"], 4 * NT * i + 4 * NT + 2)
                    chained(dve.tensor_reduce(neg_max[:, :], part_max[:, :, :], AX.X, ALU.max, negate=True), 1)
                    dve.wait_ge(s["max_turned"], i + 1)
                    for part in range(MAX_ROWS - 1):
                        chained(dve.tensor_copy(max_parts[:, part, :], neg_max[:, :]), 2 * part + 2)
                        chained(dve.tensor_tensor(neg_max[:, :], neg_max[:, :], max_parts[:, part, :],
                                                  ALU.subtract), 2 * part + 3)
                    dve.tensor_copy(max_parts[:, MAX_ROWS - 1, :], neg_max[:, :]).then_inc(s["parts_ready"], 1)
                if do_exp:
                    dve.wait_ge(s["o_turned"], h + 1)
                    o = o_ps[:, :].rearrange("p (j b e) -> p b j e", j=QB, b=QB)
                    r = rden[:, :].rearrange("p (b j) -> p b j", b=QB)
                    dve.reciprocal(r, o[:, :, :, DH]).then_inc(s["rden_done"], 1)
                    dve.wait_ge(s["rden_done"], h + 1)
                    y = c.Y[:, :, ds(h * DH, DH)].rearrange("p (b j) d -> p b j d", b=QB)
                    dve.tensor_tensor(y, o_ps[:, :].rearrange("p (j b e) -> p b j e", j=QB, b=QB)[:, :, :, 0:DH],
                                      r.unsqueeze(3).broadcast_to([P, QB, QB, DH]), ALU.mult
                                      ).then_inc(s["o_free"], 1)

            program(dve, emit)


def projection_phase(c, w_dram, bias_dram):
    nc = c.nc
    with ExitStack() as ctx:
        W = c.sb(ctx, "out_w", [P, KD, D], F32)
        bias = c.sb(ctx, "out_bias", [1, D], F32)
        ps = [c.ps(ctx, f"proj_ps{i}", [P, 512]) for i in range(2)]
        loaded = c.sem(ctx, "out_w_loaded")
        done = c.sem(ctx, "proj_done")
        copied = c.sem(ctx, "proj_copied")
        block = ctx.enter_context(nc.Block())

        @block.sync
        def _(sp):
            sp.dma_start(W[:, :, :], w_dram).then_inc(loaded, 16)
            sp.dma_start(bias[:, :], bias_dram).then_inc(loaded, 16)

        @block.tensor
        def _(pe):
            pe.wait_ge(loaded, 32)
            for t in range(NT):
                if t >= 2:
                    pe.wait_ge(copied, t - 1)
                for k in range(KD):
                    pe.matmul(ps[t % 2][:, 0:D], c.XT[:, k, t * P:(t + 1) * P], W[:, k, :], start=(k == 0),
                              stop=False)
                pe.matmul(ps[t % 2][:, 0:D], c.ones[:, :], bias[:, :], start=False, stop=True).then_inc(done, 1)

        @block.scalar
        def _(act):
            for t in range(NT):
                act.wait_ge(done, t + 1)
                act.activation(c.Y[:, t, :], ps[t % 2][:, 0:D], ACT.Copy).then_inc(copied, 1)


def turn_phase(c, tag):
    with ExitStack() as ctx:
        tp = [c.ps(ctx, f"{tag}_tp{i}", [P, 2, KD, P]) for i in range(2)]
        turned = c.sem(ctx, f"{tag}_turned")
        copied = c.sem(ctx, f"{tag}_copied")
        block = ctx.enter_context(c.nc.Block())
        transpose_tiles(c, block, c.Y, c.XT, tp, None, 0, turned, copied)


def router_phase(c, combine, gate_dram):
    nc = c.nc
    with ExitStack() as ctx:
        W = c.sb(ctx, "gate_w", [P, KD, EXPERTS], F32)
        logits = c.sb(ctx, "logits", [P, NT, EXPERTS], F32)
        best = c.sb(ctx, "best", [P, NT, 8], F32)
        best_at = c.sb(ctx, "best_at", [P, NT, 8], U32)
        at = c.sb(ctx, "best_at_f", [P, NT, 8], F32)
        iota = c.sb(ctx, "expert_no", [P, EXPERTS], F32)
        scores = c.sb(ctx, "scores", [P, NT, EXPERTS], F32)
        chosen = c.sb(ctx, "chosen", [P, 2, NT, EXPERTS], F32)
        total = c.sb(ctx, "score_sum", [P, NT], F32)
        ps = c.ps(ctx, "logit_ps", [P, NT, EXPERTS])
        loaded = c.sem(ctx, "gate_loaded")
        done = c.sem(ctx, "logits_done")
        numbered = c.sem(ctx, "numbered")
        link = c.sem(ctx, "router_link")
        shifted = c.sem(ctx, "logits_shifted")
        exped = c.sem(ctx, "scores_exped")
        block = ctx.enter_context(nc.Block())

        @block.sync
        def _(sp):
            sp.dma_start(W[:, :, :], gate_dram).then_inc(loaded, 16)

        @block.gpsimd
        def _(pool):
            pool.iota(iota[:, :], pattern=[[1, EXPERTS]], base=0, channel_multiplier=0,
                      allow_small_or_imprecise_dtypes=True).then_inc(numbered, 1)

        @block.tensor
        def _(pe):
            pe.wait_ge(loaded, 16)
            for t in range(NT):
                for k in range(KD):
                    last = pe.matmul(ps[:, t, :], c.XT[:, k, t * P:(t + 1) * P], W[:, k, :], start=(k == 0),
                                     stop=(k == KD - 1))
            last.then_inc(done, 1)

        @block.scalar
        def _(act):
            act.wait_ge(shifted, 1)
            act.activation(flat(scores[:, :, :]), flat(logits[:, :, :]), ACT.Exp).then_inc(exped, 1)

        @block.vector
        def _(dve):
            n = [0]

            def linked(ins):
                n[0] += 1
                ins.then_inc(link, 1)
                dve.wait_ge(link, n[0])

            def over_experts(ap):
                return ap.unsqueeze(2).broadcast_to([P, NT, EXPERTS])

            dve.memset(combine[:, :, EXPERTS:ALL_EXPERTS], 1.0)
            dve.wait_ge(done, 1)
            linked(dve.tensor_copy(logits[:, :, :], ps[:, :, :]))
            for t in range(NT):
                last = dve.max(best[:, t, :], logits[:, t, :])
            linked(last)
            for t in range(NT):
                last = dve.max_index(best_at[:, t, :], best[:, t, :], logits[:, t, :])
            linked(last)
            dve.tensor_copy(at[:, :, :], best_at[:, :, :])
            dve.tensor_tensor(logits[:, :, :], logits[:, :, :], over_experts(best[:, :, 0]),
                              ALU.subtract).then_inc(shifted, 1)
            dve.wait_ge(numbered, 1)
            dve.wait_ge(exped, 1)
            linked(dve.tensor_reduce(total[:, :], scores[:, :, :], AX.X, ALU.add))
            linked(dve.reciprocal(total[:, :], total[:, :]))
            for i in range(2):
                last = dve.tensor_tensor(chosen[:, i, :, :], iota[:, :].unsqueeze(1).broadcast_to([P, NT, EXPERTS]),
                                         over_experts(at[:, :, i]), ALU.is_equal)
            linked(last)
            linked(dve.tensor_tensor(chosen[:, 0, :, :], chosen[:, 0, :, :], chosen[:, 1, :, :], ALU.add))
            linked(dve.tensor_tensor(scores[:, :, :], scores[:, :, :], over_experts(total[:, :]), ALU.mult))
            dve.tensor_tensor(combine[:, :, 0:EXPERTS], scores[:, :, :], chosen[:, 0, :, :], ALU.mult)


def moe_phase(c, combine, wgu_dram, wdn_dram):
    nc = c.nc
    GROUP = 4
    groups = [range(g, min(g + GROUP, HT)) for g in range(0, HT, GROUP)]
    last_expert = [min(-(-(g[-1] + 1) * P // INTER), ALL_EXPERTS) - 1 for g in groups]
    with ExitStack() as ctx:
        wgu = c.sb(ctx, "w_gate_up", [P, KD, ALL_EXPERTS, 2 * INTER], F32)
        wdn = c.sb(ctx, "w_down", [P, HT, D], F32)
        xs = [c.sb(ctx, f"moe_x{i}", [P, KD, P], F32) for i in range(2)]
        sg = [c.sb(ctx, f"moe_silu{i}", [P, INTER], F32) for i in range(2)]
        hcat = c.sb(ctx, "hidden", [P, HT * P], F32)
        ht = c.sb(ctx, "hidden_t", [P, HT, P], F32)
        gu_ps = [c.ps(ctx, f"gu_ps{i}", [P, 512]) for i in range(3)]
        tp = [c.ps(ctx, f"hidden_tp{i}", [P, GROUP, P]) for i in range(2)]
        y_ps = c.ps(ctx, "moe_y_ps", [P, 512])
        s = {n: c.sem(ctx, n) for n in (
            "wgu_in", "wdn_in", "moe_x_ready", "moe_x_free", "pad_zeroed", "gu_done", "silu_done", "gu_free",
            "hidden_turned", "hidden_copied", "y_done", "y_free")}
        block = ctx.enter_context(nc.Block())

        @block.sync
        def _(sp):
            for e in range(0, ALL_EXPERTS, 3):
                sp.dma_start(wgu[:, :, e:e + 3, :], wgu_dram[:, :, e:e + 3, :]).then_inc(s["wgu_in"], 16)
            sp.dma_start(wdn[:, :, :], wdn_dram).then_inc(s["wdn_in"], 16)

        @block.gpsimd
        def _(pool):
            pool.sem_inc(s["moe_x_free"], 2)
            pool.memset(hcat[:, HCAT:HT * P], 0.0).then_inc(s["pad_zeroed"], 1)
            with pool.Fori(0, NT // 2) as i:
                for j in range(2):
                    t = 2 * i + j
                    pool.wait_ge(s["moe_x_free"], t + 1)
                    pool.tensor_copy(xs[j][:, :, :], c.XT[:, :, ds(t * P, P)]).then_inc(s["moe_x_ready"], 1)

        @block.tensor
        def _(pe):
            pe.sem_inc(s["gu_free"], 3)
            pe.sem_inc(s["hidden_copied"], 2)
            pe.wait_ge(s["wgu_in"], 16 * (ALL_EXPERTS // 3))
            pe.wait_ge(s["wdn_in"], 16)
            pe.wait_ge(s["pad_zeroed"], 1)

            def up(t, x, e):
                pe.wait_ge(s["gu_free"], ALL_EXPERTS * t + e + 1)
                for k in range(KD):
                    last = pe.matmul(gu_ps[e % 3][:, 0:2 * INTER], x[:, k, :], wgu[:, k, e, :], start=(k == 0),
                                     stop=(k == KD - 1))
                last.then_inc(s["gu_done"], 1)

            def turn(t, g):
                pe.wait_ge(s["gu_free"], ALL_EXPERTS * t + last_expert[g] + 1 + 3)
                pe.wait_ge(s["hidden_copied"], len(groups) * t + g + 1)
                for n, k in enumerate(groups[g]):
                    last = pe.transpose(tp[g % 2][:, n, :], hcat[:, k * P:(k + 1) * P], c.ident[:, :])
                last.then_inc(s["hidden_turned"], 1)

            def down(t, g):
                pe.wait_ge(s["hidden_copied"], len(groups) * t + g + 1 + 2)
                if g == 0:
                    pe.wait_ge(s["y_free"], t + 1)
                for k in groups[g]:
                    last = pe.matmul(y_ps[:, 0:D], ht[:, k, :], wdn[:, k, :], start=(k == 0), stop=(k == HT - 1))
                if g == len(groups) - 1:
                    last.then_inc(s["y_done"], 1)

            with pe.Fori(0, NT // 2) as i:
                for j in range(2):
                    t = 2 * i + j
                    pe.wait_ge(s["moe_x_ready"], t + 1)
                    turned = downed = 0
                    for e in range(ALL_EXPERTS + 2):
                        if e < ALL_EXPERTS:
                            up(t, xs[j], e)
                        if downed < turned:
                            down(t, downed)
                            downed += 1
                        if turned < len(groups) and last_expert[turned] <= e - 2:
                            turn(t, turned)
                            turned += 1
                    while downed < len(groups):
                        if turned < len(groups):
                            turn(t, turned)
                            turned += 1
                        down(t, downed)
                        downed += 1

        @block.scalar
        def _(act):
            with act.Fori(0, NT // 2) as i:
                for j in range(2):
                    t = 2 * i + j
                    for e in range(ALL_EXPERTS):
                        n = ALL_EXPERTS * t + e
                        act.wait_ge(s["gu_done"], n + 1)
                        act.wait_ge(s["gu_free"], n + 2)
                        act.activation(sg[e % 2][:, :], gu_ps[e % 3][:, 0:INTER], ACT.Silu
                                       ).then_inc(s["silu_done"], 1)

        @block.vector
        def _(dve):
            dve.sem_inc(s["y_free"], 1)

            def copy_hidden(t, g):
                dve.wait_ge(s["hidden_turned"], len(groups) * t + g + 1)
                n = len(groups[g])
                dve.tensor_copy(ht[:, groups[g][0]:groups[g][-1] + 1, :], tp[g % 2][:, 0:n, :]
                                ).then_inc(s["hidden_copied"], 1)

            with dve.Fori(0, NT // 2) as i:
                for j in range(2):
                    t = 2 * i + j
                    copied = 0
                    for e in range(ALL_EXPERTS):
                        n = ALL_EXPERTS * t + e
                        if e == 0:
                            dve.wait_ge(s["y_free"], t + 1)
                        dve.wait_ge(s["silu_done"], n + 1)
                        dve.scalar_tensor_tensor(
                            hcat[:, e * INTER:(e + 1) * INTER], sg[e % 2][:, :],
                            combine[:, ds(t, 1), e:e + 1].rearrange("p a b -> p (a b)"),
                            gu_ps[e % 3][:, INTER:2 * INTER], ALU.mult, ALU.mult).then_inc(s["gu_free"], 1)
                        if copied < len(groups) and last_expert[copied] <= e - 2:
                            copy_hidden(t, copied)
                            copied += 1
                    for g in range(copied, len(groups)):
                        copy_hidden(t, g)
                    dve.wait_ge(s["y_done"], t + 1)
                    dve.tensor_copy(c.Y[:, ds(t, 1), :].rearrange("p a d -> p (a d)"), y_ps[:, 0:D]
                                    ).then_inc(s["y_free"], 1)
                    dve.sem_inc(s["moe_x_free"], 1)


def ffn_phase(c, wg_dram, wu_dram, wd_dram, gs_dram, us_dram, ds_dram):
    nc = c.nc
    NB, B = 4, T // 4
    ZERO_POINT = 128.0
    with ExitStack() as ctx:
        wq = c.sb(ctx, "ffn_int", [P, 3, 2 * FFN], I32)
        w = c.sb(ctx, "ffn_w", [P, 3, 2 * FFN], F32)
        scale = c.sb(ctx, "ffn_scales", [P, 2, FT], F32)
        out_scale = c.sb(ctx, "ffn_out_scale", [P, D], F32)
        sg = [c.sb(ctx, f"ffn_silu{i}", [P, B], F32) for i in range(2)]
        ht = [c.sb(ctx, f"ffn_hidden{i}", [P, FT, B], F32) for i in range(2)]
        g_ps = [c.ps(ctx, f"g_ps{i}", [P, B]) for i in range(2)]
        u_ps = [c.ps(ctx, f"u_ps{i}", [P, B]) for i in range(2)]
        y_ps = [c.ps(ctx, f"ffn_y_ps{i}", [P, 512]) for i in range(2)]
        s = {n: c.sem(ctx, n) for n in (
            "ffn_in", "dequantised", "g_done", "u_done", "ffn_silu_done", "hidden_done", "ffn_y_done", "ffn_y_free")}
        wg = w[:, 0, :].rearrange("p (k n) -> p k n", k=KD)
        wu = w[:, 1, :].rearrange("p (k n) -> p k n", k=KD)
        wd = w[:, 2, :].rearrange("p (k n) -> p k n", k=FT)
        block = ctx.enter_context(nc.Block())

        @block.sync
        def _(sp):
            for i, src in enumerate((wg_dram, wu_dram, wd_dram)):
                sp.dma_start(wq[:, i, :], src).then_inc(s["ffn_in"], 16)
            sp.dma_start(scale[:, 0, :], gs_dram).then_inc(s["ffn_in"], 16)
            sp.dma_start(scale[:, 1, :], us_dram).then_inc(s["ffn_in"], 16)
            sp.dma_start(out_scale[:, :], ds_dram.broadcast_to([P, D])).then_inc(s["ffn_in"], 16)

        @block.tensor
        def _(pe):
            pe.sem_inc(s["hidden_done"], 2)
            pe.sem_inc(s["ffn_y_free"], 2)
            pe.wait_ge(s["dequantised"], 3)
            with pe.Fori(0, NB // 2) as i:
                for j in range(2):
                    b = 2 * i + j
                    for m in range(FT):
                        pe.wait_ge(s["hidden_done"], FT * b + m + 1)
                        for weights, ps, done in ((wg, g_ps, "g_done"), (wu, u_ps, "u_done")):
                            for k in range(KD):
                                last = pe.matmul(ps[m % 2][:, :], weights[:, k, m * P:(m + 1) * P],
                                                 c.XT[:, k, ds(b * B, B)], start=(k == 0), stop=(k == KD - 1))
                            last.then_inc(s[done], 1)
                    for q in range(B // P):
                        pe.wait_ge(s["hidden_done"], FT * b + FT + 2)
                        pe.wait_ge(s["ffn_y_free"], (B // P) * b + q + 1)
                        for m in range(FT):
                            last = pe.matmul(y_ps[q % 2][:, 0:D], ht[j][:, m, q * P:(q + 1) * P], wd[:, m, :],
                                             start=(m == 0), stop=(m == FT - 1))
                        last.then_inc(s["ffn_y_done"], 1)

        @block.scalar
        def _(act):
            act.wait_ge(s["ffn_in"], 96)
            with act.Fori(0, NB // 2) as i:
                for j in range(2):
                    for m in range(FT):
                        n = FT * (2 * i + j) + m
                        act.wait_ge(s["g_done"], n + 1)
                        act.wait_ge(s["hidden_done"], n + 1)
                        act.activation(sg[m % 2][:, :], g_ps[m % 2][:, :], ACT.Silu, scale=scale[:, 0, m:m + 1]
                                       ).then_inc(s["ffn_silu_done"], 1)

        @block.vector
        def _(dve):
            dve.wait_ge(s["ffn_in"], 96)
            for i in range(3):
                dve.tensor_scalar(w[:, i, :], wq[:, i, :], ZERO_POINT, None, ALU.subtract
                                  ).then_inc(s["dequantised"], 1)
            with dve.Fori(0, NB // 2) as i:
                for j in range(2):
                    b = 2 * i + j
                    for m in range(FT):
                        n = FT * b + m
                        dve.wait_ge(s["ffn_silu_done"], n + 1)
                        dve.wait_ge(s["u_done"], n + 1)
                        dve.scalar_tensor_tensor(ht[j][:, m, :], u_ps[m % 2][:, :], scale[:, 1, m:m + 1],
                                                 sg[m % 2][:, :], ALU.mult, ALU.mult).then_inc(s["hidden_done"], 1)
                    for q in range(B // P):
                        dve.wait_ge(s["ffn_y_done"], (B // P) * b + q + 1)
                        dve.tensor_tensor(c.Y[:, ds((B // P) * b + q, 1), :].rearrange("p a d -> p (a d)"),
                                          y_ps[q % 2][:, 0:D], out_scale[:, :], ALU.mult
                                          ).then_inc(s["ffn_y_free"], 1)


HK, HV, DK = 16, 32, 128
VH = HV // HK
KCONV = 4
QC = 4
QT_ = QC * P
NQ = NT // QC
NM = QC * VH
GM = NM // 2
CH = 2 + VH
BLOCK = 16
EPS = 1e-6
TINY = 1e-18
GRID = 1e-11
W_CONV = KD * (CH + VH) * DK
W_OUT = W_CONV + CH * KCONV
W_ALL = W_OUT + VH * D

UNITS = ["b", "im", "a2", "b2", "y2", "a4", "b4", "y3", "b8", "y4",
         "r0", "x0", "n0", "r1", "x1", "n1", "r2", "x2", "n2"]
BY_DVE = {"im", "a2", "b2", "a4", "b4", "y2", "y3", "y4", "r0", "r1", "r2", "n0", "n1", "n2"}
NU = len(UNITS)
NU_DVE = len(BY_DVE)
NU_ACT = NU - NU_DVE


def copied_by(name):
    i = UNITS.index(name)
    mine = name in BY_DVE
    return mine, sum((u in BY_DVE) == mine for u in UNITS[:i + 1])


def delta_tables(c, tab, a):
    nc = c.nc
    with ExitStack() as ctx:
        W = c.sb(ctx, "w_ab", [P, KD, 2 * HV], F32)
        bias = c.sb(ctx, "gate_bias", [P, 2, HV], F32)
        y = c.sb(ctx, "gate_y", [P, NT, HV], F32)
        tmp = c.sb(ctx, "gate_tmp", [P, NT, HV], F32)
        ab = [c.ps(ctx, f"ab_ps{i}", [P, NT // 2, 2 * HV]) for i in range(2)]
        sums = [c.ps(ctx, f"sum_ps{i}", [P, NT, HV]) for i in range(3)]
        s = {n: c.sem(ctx, n) for n in ("ab_in", "ab_done", "gate_link", "act_link", "summed", "masks_done")}
        block = ctx.enter_context(nc.Block())

        @block.sync
        def _(sp):
            sp.dma_start(W[:, :, :], a["w_ab"]).then_inc(s["ab_in"], 16)
            sp.dma_start(bias[:, 0, :], a["dt_bias"].broadcast_to([P, HV])).then_inc(s["ab_in"], 16)
            sp.dma_start(bias[:, 1, :], a["a_log"].broadcast_to([P, HV])).then_inc(s["ab_in"], 16)
            sp.dma_start(tab["norm_w"], a["norm_w"].broadcast_to([P, DK])).then_inc(s["ab_in"], 16)

        @block.gpsimd
        def _(pool):
            n = [0]

            def linked(ins):
                n[0] += 1
                ins.then_inc(s["masks_done"], 1)
                pool.wait_ge(s["masks_done"], n[0])

            for name in ("upto", "after", "before", "block"):
                linked(pool.memset(tab[name], 1.0))
            linked(pool.memset(tab["neg"], -30000.0))
            linked(pool.memset(tab["ones"], 1.0))
            linked(pool.memset(tab["halo"], 1.0))
            linked(pool.memset(tab["half"], 0.5))
            linked(pool.memset(tab["mhalf"], -0.5))
            linked(pool.memset(tab["halo"][:, 0:1], 0.0))
            sel = lambda ap, pattern, base, mult, op: linked(pool.affine_select(
                out=ap, in_=ap, compare_op=op, fill=0.0, base=base, pattern=pattern, channel_multiplier=mult))
            sel(tab["upto"], [[1, P]], 0, -1, ALU.is_ge)
            sel(tab["after"], [[-1, P]], 0, 1, ALU.is_gt)
            sel(tab["before"], [[1, P]], 0, -1, ALU.is_gt)
            sel(tab["neg"], [[-1, P]], 0, 1, ALU.is_gt)
            blocks = tab["block"].rearrange("p (b c) -> p b c", c=BLOCK)
            sel(tab["block"], [[1, P]], 0, -1, ALU.is_gt)
            sel(blocks, [[-BLOCK, P // BLOCK], [0, BLOCK]], 0, 1, ALU.is_ge)
            sel(blocks, [[BLOCK, P // BLOCK], [0, BLOCK]], BLOCK - 1, -1, ALU.is_ge)

        @block.tensor
        def _(pe):
            pe.wait_ge(s["ab_in"], 64)
            for t in range(NT):
                for k in range(KD):
                    last = pe.matmul(ab[t // 8][:, t % 8, :], c.XT[:, k, t * P:(t + 1) * P], W[:, k, :],
                                     start=(k == 0), stop=(k == KD - 1))
            last.then_inc(s["ab_done"], 1)
            pe.wait_ge(s["masks_done"], 17)
            pe.wait_ge(s["gate_link"], 7)
            for i, m in enumerate(("upto", "after", "ones")):
                last = pe.matmul(flat(sums[i][:, :, :]), tab[m], flat(tab["g"]), start=True, stop=True)
            last.then_inc(s["summed"], 1)

        @block.scalar
        def _(act):
            def linked(ins, n):
                ins.then_inc(s["act_link"], 1)
                act.wait_ge(s["act_link"], n)

            act.wait_ge(s["ab_in"], 64)
            linked(act.activation(bias[:, 1, :], bias[:, 1, :], ACT.Exp), 1)
            act.wait_ge(s["gate_link"], 3)
            linked(act.activation(flat(tmp[:, :, :]), flat(tmp[:, :, :]), ACT.Exp), 2)
            linked(act.activation(flat(tab["nbeta"]), flat(tab["nbeta"]), ACT.Exp), 3)
            linked(act.activation(flat(tmp[:, :, :]), flat(tmp[:, :, :]), ACT.Ln, bias=1.0), 4)
            act.wait_ge(s["summed"], 1)
            for i, name in enumerate(("neg_decay", "decay_after", "chunk_decay")):
                linked(act.activation(flat(tab[name]), flat(sums[i][:, :, :]), ACT.Exp), 5 + i)

        @block.vector
        def _(dve):
            def linked(ins, n):
                ins.then_inc(s["gate_link"], 1)
                dve.wait_ge(s["gate_link"], n)

            heads = lambda ap: ap.unsqueeze(1).broadcast_to([P, NT, HV])
            dve.wait_ge(s["ab_done"], 1)
            for i in range(2):
                half = slice(8 * i, 8 * i + 8)
                dve.tensor_scalar(tab["nbeta"][:, half, :], ab[i][:, :, 0:HV], -1.0, None, ALU.mult)
                last = dve.tensor_tensor(y[:, half, :], ab[i][:, :, HV:2 * HV],
                                         bias[:, 0, :].unsqueeze(1).broadcast_to([P, 8, HV]), ALU.add)
            linked(last, 1)
            linked(dve.tensor_scalar(tmp[:, :, :], y[:, :, :], -1.0, None, ALU.mult), 2)
            linked(dve.tensor_tensor(tmp[:, :, :], tmp[:, :, :], y[:, :, :], ALU.min), 3)
            dve.wait_ge(s["act_link"], 4)
            linked(dve.scalar_tensor_tensor(y[:, :, :], y[:, :, :], 0.0, tmp[:, :, :], ALU.max, ALU.add), 4)
            dve.tensor_scalar(tab["nbeta"], tab["nbeta"], 1.0, None, ALU.add)
            linked(dve.tensor_scalar(y[:, :, :], y[:, :, :], -1.0, None, ALU.mult), 5)
            linked(dve.tensor_tensor(tab["g"], y[:, :, :], heads(bias[:, 1, :]), ALU.mult), 6)
            linked(dve.reciprocal(tab["nbeta"], tab["nbeta"]), 7)
            linked(dve.tensor_scalar(tab["nbeta"], tab["nbeta"], -1.0, None, ALU.mult), 8)
            dve.wait_ge(s["act_link"], 7)
            linked(dve.tensor_scalar(tab["neg_decay"], tab["neg_decay"], -1.0, None, ALU.mult), 9)
            dve.memset(tab["neg_decay"][:, 0, :], 0.0)
            dve.memset(tab["chunk_decay"][:, 0, :], 0.0)
            dve.tensor_scalar(tab["norm_w"], tab["norm_w"], -1.0, None, ALU.mult)


def delta_phase(c, a):
    nc = c.nc
    with ExitStack() as outer:
        f = lambda name, shape, dt=F32: c.sb(outer, "t_" + name, shape, dt)
        tab = {}
        for name in ("g", "nbeta", "neg_decay", "decay_after", "chunk_decay"):
            tab[name] = f(name, [P, NT, HV])[:, :, :]
        for name in ("upto", "after", "before", "block", "ones", "norm_w"):
            tab[name] = f(name, [P, P])[:, :]
        tab["neg"] = f("neg", [P, P], BF16)[:, :]
        tab["halo"] = f("halo", [P, NQ])[:, :]
        tab["half"] = f("half", [P, NM])[:, :]
        tab["mhalf"] = f("mhalf", [P, NM])[:, :]
        delta_tables(c, tab, a)
        delta_heads(c, tab, a)


def delta_heads(c, tab, a):
    nc = c.nc
    with ExitStack() as ctx:
        f = lambda name, shape, dt=F32: c.sb(ctx, "dl_" + name, shape, dt)
        landing = f("landing", [P, W_ALL])
        ws = f("weights", [P, W_ALL])
        wqkvz = ws[:, 0:W_CONV].rearrange("p (k m n) -> p k m n", k=KD, n=DK)
        conv_w = ws[:, W_CONV:W_OUT].rearrange("p (m k) -> p m k", k=KCONV)
        w_out = ws[:, W_OUT:W_ALL].rearrange("p (a n) -> p a n", a=VH)
        xs = f("x", [P, KD, QT_])
        raw = f("raw", [P, CH, KCONV - 1 + QT_])
        cv = f("conv", [P, CH, QT_])
        kq = f("kq", [P, 2, QT_])
        vt = f("vt", [P, VH, QT_])
        zs = f("z", [P, QC, VH, DK])
        zn = f("z_normed", [P, QC, VH, DK])
        kt = f("k_tok", [P, QC, DK])
        junk = f("junk", [P, 12, DK])
        sumsq = f("sumsq", [P, 2, QC])
        nsq = f("nsq", [P, QC])
        norm_k = f("norm_k", [P, QC])
        rn = f("inv_nsq", [P, QC])
        sn = f("s", [P, QC, VH])
        snd = f("s_decayed", [P, QC, VH])
        nd = f("neg_decay_q", [P, QC, VH])
        cd = f("chunk_decay_q", [P, QC, VH])
        qe = f("q_eps", [P, QC])
        vr = f("v_scaled", [P, QC, VH, DK])
        gu = f("g_upto", [P, NM, P])
        gam = [f(f"gamma{g}", [P, GM, P]) for g in range(2)]
        attn = [f(f"attn{g}", [P, GM, P]) for g in range(2)]
        ln = [f(f"l_raw{g}", [P, GM, P]) for g in range(2)]
        lm = [f(f"l{g}", [P, GM, P]) for g in range(2)]
        buf = [{n: f(f"{n}_{g}", [P, GM, P]) for n in ("a", "b", "im", "a2", "b2", "a4", "b4", "b8", "ya", "yb",
                                                       "x", "f")} for g in range(2)]
        eye2 = f("two_ident", [P, P])
        S = f("state", [P, VH, DK])
        r0 = f("r", [P, VH, DK])
        v2 = f("v2", [P, VH, DK])
        v3 = f("v3", [P, VH, DK])
        tq = [f(f"q_state{i}", [P, VH, DK]) for i in range(2)]
        on = [f(f"core{i}", [P, VH, DK]) for i in range(2)]
        ms = [f(f"meansq{i}", [P, VH]) for i in range(2)]
        osc = [f(f"out_scale{i}", [P, VH]) for i in range(2)]
        gated = [f(f"gated{i}", [P, VH, DK]) for i in range(2)]
        gt = [f(f"gated_t{i}", [P, VH, P]) for i in range(2)]
        prep = [c.ps(ctx, f"prep{i}", [P, 4, P]) for i in range(2)]
        inv = [[c.ps(ctx, f"inv{g}{i}", [P, GM, P]) for i in range(2)] for g in range(2)]
        ra = c.ps(ctx, "rec_a", [P, 2, VH, DK])
        rb = c.ps(ctx, "rec_b", [P, 2, VH, DK])
        names = ("halo_done", "flushed", "y4_sum", "w_landed", "w_ready", "w_taken", "x_ready", "raw_done", "raw_free", "conv_step", "silu_done",
                 "prep_mm", "prep_act", "prep_dve", "zn_done", "sq_k", "scal", "nsq_done", "norm_done", "gu_done",
                 "lraw_done", "masked", "y1_done", "inv_mm0", "inv_mm1", "inv_act0", "inv_act1", "inv_dve0",
                 "inv_dve1", "ks_done", "r_done", "tq_done", "u_done", "v3_done", "v2_done", "sv_done", "av_done",
                 "s_done", "o_done", "o_sq", "osc_link", "osc_done", "gated_done", "gt_done", "gt_copied",
                 "y_done", "y_added", "quad_done", "zeroed")
        s = {n: c.sem(ctx, "dn_" + n) for n in names}
        block = ctx.enter_context(nc.Block())
        OPERANDS = {"a2": ("b", "a"), "b2": ("a", "b"), "y2": ("b2", "ya"), "a4": ("b2", "a2"), "b4": ("a2", "b2"),
                    "y3": ("b4", "yb"), "b8": ("a4", "b4"), "y4": ("b8", "ya"),
                    "r0": ("im", "yb"), "n0": ("x", "f"), "r1": ("im", "ya"), "n1": ("x", "f"),
                    "r2": ("im", "yb"), "n2": ("x", "f")}
        TURNS = {"b": "a", "x0": "yb", "x1": "ya", "x2": "yb"}
        OUT = {"b": "b", "im": "im", "a2": "a2", "b2": "b2", "y2": "yb", "a4": "a4", "b4": "b4", "y3": "ya",
               "b8": "b8", "y4": "yb", "r0": "f", "x0": "x", "n0": "ya", "r1": "f", "x1": "x", "n1": "yb",
               "r2": "f", "x2": "x", "n2": "ya"}
        NEEDS = {"a2": ["b"], "b2": ["b"], "y2": ["b2"], "a4": ["b2", "a2"], "b4": ["a2", "b2"], "y3": ["b4", "y2"],
                 "b8": ["a4", "b4"], "y4": ["b8", "y3"], "r0": ["im", "y4"], "x0": ["y4"], "n0": ["r0", "x0"],
                 "r1": ["n0"], "x1": ["n0"], "n1": ["r1", "x1"], "r2": ["n1"], "x2": ["n1"], "n2": ["r2", "x2"]}
        FINAL = "ya"

        def copied(engine, g, names, n):
            by = [copied_by(name) for name in names]
            dve = max([k for mine, k in by if mine], default=0)
            act = max([k for mine, k in by if not mine], default=0)
            if dve:
                engine.wait_ge(s[f"inv_dve{g}"], NU_DVE * n + dve)
            if act:
                engine.wait_ge(s[f"inv_act{g}"], NU_ACT * n + act)

        def over_quads(engine, emit, head=None):
            with engine.Fori(0, HK) as kh:
                if head:
                    head(kh)
                with engine.Fori(0, NQ) as q:
                    emit(kh, q, NQ * kh + q)

        @block.sync
        def _(sp):
            sp.sem_inc(s["w_taken"], 1)
            with sp.Fori(0, HK) as kh:
                sp.wait_ge(s["w_taken"], kh + 1)
                sp.dma_start(landing[:, :], a["w_delta"][ds(kh, 1), :, :].rearrange("a p n -> (a p) n")
                             ).then_inc(s["w_landed"], 16)

        @block.tensor
        def _(pe):
            pe.sem_inc(s["prep_act"], 10)
            pe.sem_inc(s["prep_dve"], 4)
            pe.sem_inc(s["s_done"], 1)
            pe.sem_inc(s["gt_copied"], 4)
            pe.sem_inc(s["y_added"], 4)
            pe.wait_ge(s["zeroed"], 1)

            def prep_unit(n, u, mms):
                if u in (0, 1):
                    pe.wait_ge(s["prep_dve"], 4 * n + 3 + u)
                elif u in (10, 11):
                    pe.wait_ge(s["prep_dve"], 4 * n + 4 + u - 9)
                elif u in (12, 13):
                    pe.wait_ge(s["prep_act"], 10 * n + 10 + u - 3)
                else:
                    pe.wait_ge(s["prep_act"], 10 * n + 10 + u - 1)
                mms(prep[u % 2]).then_inc(s["prep_mm"], 1)

            def emit(kh, q, n):
                pe.wait_ge(s["w_ready"], kh + 1)
                pe.wait_ge(s["x_ready"], n + 1)
                pe.wait_ge(s["gt_copied"], 4 * n + 4)
                pe.wait_ge(s["y_added"], 4 * n + 4)
                for m in range(CH):
                    def project(bank, m=m):
                        for k in range(KD):
                            last = pe.matmul(flat(bank[:, :, :]), wqkvz[:, k, m, :], xs[:, k, :], start=(k == 0),
                                             stop=(k == KD - 1))
                        return last
                    prep_unit(n, m, project)
                for i in range(2):
                    def project_z(bank, i=i):
                        for j in range(2):
                            for k in range(KD):
                                last = pe.matmul(flat(bank[:, 2 * j:2 * j + 2, :]),
                                                 xs[:, k, (2 * i + j) * P:(2 * i + j + 1) * P],
                                                 flat(wqkvz[:, k, CH:CH + VH, :]), start=(k == 0),
                                                 stop=(k == KD - 1))
                        return last
                    prep_unit(n, 4 + i, project_z)
                for i in range(2):
                    pe.wait_ge(s["silu_done"], 4 * n + 2)

                    def turn_kq(bank, i=i):
                        for j in range(2):
                            for x in range(2):
                                last = pe.transpose(bank[:, 2 * j + x, :], kq[:, x, (2 * i + j) * P:(2 * i + j + 1) * P],
                                                    c.ident[:, :])
                        return last
                    prep_unit(n, 6 + i, turn_kq)
                for i in range(2):
                    pe.wait_ge(s["silu_done"], 4 * n + 4)

                    def turn_v(bank, i=i):
                        for j in range(2):
                            for h in range(VH):
                                last = pe.transpose(bank[:, 2 * j + h, :], vt[:, h, (2 * i + j) * P:(2 * i + j + 1) * P],
                                                    c.ident[:, :])
                        return last
                    prep_unit(n, 8 + i, turn_v)
                for g in range(2):
                    pe.wait_ge(s["gu_done"], n + 1)

                    def decays(bank, g=g):
                        pe.matmul(flat(bank[:, :, :]), tab["after"], flat(gu[:, GM * g:GM * g + GM, :]),
                                  start=True, stop=False)
                        return pe.matmul(bank[:, :, :], c.identb[:, :],
                                         tab["neg"].unsqueeze(1).broadcast_to([P, GM, P]), start=False, stop=True)
                    prep_unit(n, 10 + g, decays)
                for i in range(2):
                    def products(bank, i=i):
                        for j in range(2):
                            cols = slice((2 * i + j) * P, (2 * i + j + 1) * P)
                            last = pe.matmul(bank[:, 2 * j:2 * j + 2, :], kq[:, 0, cols], kq[:, :, cols],
                                             start=True, stop=True)
                        return last
                    prep_unit(n, 12 + i, products)

                def unit(g, u):
                    name, B = UNITS[u], buf[g]
                    copied(pe, g, NEEDS.get(name, []) + UNITS[max(u - 2, 0):max(u - 1, 0)], n)
                    if name == "b":
                        pe.wait_ge(s["masked"], 4 * n + 2 * g + 1)
                    if name == "im":
                        pe.wait_ge(s["masked"], 4 * n + 2 * g + 2)
                    if name == "y2":
                        pe.wait_ge(s["y1_done"], 2 * n + g + 1)
                    bank = inv[g][u % 2]
                    for m in range(GM):
                        if name == "im":
                            last = pe.transpose(bank[:, m, :], lm[g][:, m, :], c.ident[:, :])
                        elif name in TURNS:
                            last = pe.transpose(bank[:, m, :], B[TURNS[name]][:, m, :], c.ident[:, :])
                        else:
                            w, x = OPERANDS[name]
                            last = pe.matmul(bank[:, m, :], B[w][:, m, :], B[x][:, m, :], start=True, stop=True)
                    last.then_inc(s[f"inv_mm{g}"], 1)

                for u in range(NU):
                    for g in range(2):
                        unit(g, u)
                for g in range(2):
                    copied(pe, g, ["n2"], n)

                def recur(ch):
                    m = QC * n + ch
                    cols = slice(ch * P, (ch + 1) * P)
                    g, j = ch // 2, VH * (ch % 2)
                    pe.wait_ge(s["s_done"], m + 1)
                    pe.matmul(flat(ra[:, 0, :, :]), kq[:, 0, cols], flat(S[:, :, :]), start=True, stop=True)
                    pe.matmul(flat(ra[:, 1, :, :]), kq[:, 1, cols], flat(S[:, :, :]), start=True, stop=True
                              ).then_inc(s["ks_done"], 1)
                    pe.wait_ge(s["r_done"], m + 1)
                    for h in range(VH):
                        last = pe.matmul(rb[:, 0, h, :], buf[g][FINAL][:, j + h, :], r0[:, h, :], start=True, stop=True)
                    last.then_inc(s["u_done"], 1)
                    pe.wait_ge(s["v3_done"], m + 1)
                    pe.wait_ge(s["tq_done"], m + 1)
                    pe.matmul(flat(ra[:, 0, :, :]), kt[:, ch, :], flat(v3[:, :, :]), start=True, stop=True
                              ).then_inc(s["sv_done"], 1)
                    pe.wait_ge(s["v2_done"], m + 1)
                    for h in range(VH):
                        last = pe.matmul(rb[:, 1, h, :], attn[g][:, j + h, :], v2[:, h, :], start=True, stop=True)
                    last.then_inc(s["av_done"], 1)

                def output(ch):
                    m = QC * n + ch
                    pe.wait_ge(s["gated_done"], m + 1)
                    pe.wait_ge(s["gt_copied"], m + 4)
                    for h in range(VH):
                        last = pe.transpose(prep[0][:, h, :], gated[ch % 2][:, h, :], c.ident[:, :])
                    last.then_inc(s["gt_done"], 1)
                    pe.wait_ge(s["gt_copied"], m + 5)
                    pe.wait_ge(s["y_added"], m + 4)
                    for h in range(VH):
                        last = pe.matmul(flat(prep[1][:, 0:2, :]), gt[ch % 2][:, h, :], w_out[:, h, :],
                                         start=(h == 0), stop=(h == VH - 1))
                    last.then_inc(s["y_done"], 1)

                for ch in range(QC):
                    recur(ch)
                    if ch:
                        output(ch - 1)
                output(QC - 1)

            over_quads(pe, emit)

        @block.scalar
        def _(act):
            act.sem_inc(s["quad_done"], 1)
            act.wait_ge(s["zeroed"], 1)

            def emit(kh, q, n):
                act.wait_ge(s["raw_free"], n + 1)
                act.activation(raw[:, :, 0:KCONV - 1], raw[:, :, QT_:QT_ + KCONV - 1], ACT.Copy,
                               scale=tab["halo"][:, ds(q, 1)]).then_inc(s["halo_done"], 1)
                act.wait_ge(s["halo_done"], n + 1)
                for m in range(CH):
                    act.wait_ge(s["prep_mm"], 14 * n + m + 1)
                    act.activation(raw[:, m, KCONV - 1:], flat(prep[m % 2][:, :, :]), ACT.Copy
                                   ).then_inc(s["prep_act"], 1)
                act.wait_ge(s["zn_done"], n + 1)
                for i in range(2):
                    act.wait_ge(s["prep_mm"], 14 * n + 5 + i)
                    act.activation(flat(zs[:, 2 * i:2 * i + 2, :, :]), flat(prep[i][:, :, :]), ACT.Silu
                                   ).then_inc(s["prep_act"], 1)
                act.wait_ge(s["quad_done"], n + 1)
                for m, dst in enumerate((kq[:, 1, :], kq[:, 0, :], vt[:, 0, :], vt[:, 1, :])):
                    act.wait_ge(s["conv_step"], 16 * n + 13 + m)
                    act.activation(dst, cv[:, m, :], ACT.Silu).then_inc(s["silu_done"], 1)
                for i in range(2):
                    act.wait_ge(s["prep_mm"], 14 * n + 7 + i)
                    bank = prep[i][:, :, :].rearrange("p (j x) d -> p j x d", x=2)
                    for j in range(2):
                        for x in range(2):
                            last = act.activation(junk[:, 4 * i + 2 * j + x, :], bank[:, j, x, :], ACT.Square,
                                                  accum_out=sumsq[:, x, 2 * i + j:2 * i + j + 1])
                    last.then_inc(s["sq_k"], 1)
                    act.activation(kt[:, 2 * i:2 * i + 2, :], bank[:, :, 0, :], ACT.Copy).then_inc(s["prep_act"], 1)
                for g in range(2):
                    act.wait_ge(s["prep_mm"], 14 * n + 11 + g)
                    act.activation(flat(gam[g][:, :, :]), flat(prep[g][:, :, :]), ACT.Exp).then_inc(s["prep_act"], 1)

                def unit(g, u):
                    name = UNITS[u]
                    if name in BY_DVE:
                        return
                    act.wait_ge(s[f"inv_mm{g}"], NU * n + u + 1)
                    act.activation(flat(buf[g][OUT[name]][:, :, :]), flat(inv[g][u % 2][:, :, :]), ACT.Copy
                                   ).then_inc(s[f"inv_act{g}"], 1)

                for u in range(NU):
                    for g in range(2):
                        unit(g, u)

                def output(ch):
                    m = QC * n + ch
                    act.wait_ge(s["o_done"], m + 1)
                    for h in range(VH):
                        last = act.activation(junk[:, 8 + 2 * (ch % 2) + h, :], on[ch % 2][:, h, :], ACT.Square,
                                              accum_out=ms[ch % 2][:, h:h + 1])
                    last.then_inc(s["o_sq"], 1)
                    act.wait_ge(s["o_sq"], m + 1)
                    act.activation(osc[ch % 2][:, :], ms[ch % 2][:, :], ACT.Identity, scale=1.0 / DK,
                                   bias=qe[:, ch:ch + 1]).then_inc(s["osc_link"], 1)
                    act.wait_ge(s["gt_done"], m + 1)
                    act.activation(flat(gt[ch % 2][:, :, :]), flat(prep[0][:, 0:VH, :]), ACT.Copy
                                   ).then_inc(s["gt_copied"], 1)

                for ch in range(QC):
                    m = QC * n + ch
                    act.wait_ge(s["r_done"], m + 1)
                    for h in range(VH):
                        last = act.activation(tq[ch % 2][:, h, :], ra[:, 1, h, :], ACT.Copy,
                                              scale=nd[:, ch, h:h + 1])
                    last.then_inc(s["tq_done"], 1)
                    if ch:
                        output(ch - 1)
                output(QC - 1)

            over_quads(act, emit)

        @block.gpsimd
        def _(pool):
            pool.sem_inc(s["zn_done"], 1)

            def emit(kh, q, n):
                pool.wait_ge(s["quad_done"], n + 1)
                pool.tensor_copy(xs[:, :, :], c.XT[:, :, ds(QT_ * q, QT_)]).then_inc(s["x_ready"], 1)
                gsl = tab["g"][:, ds(QC * q, QC), ds(VH * kh, VH)].unsqueeze(3).broadcast_to([P, QC, VH, P])
                mask = tab["upto"].unsqueeze(1).unsqueeze(1).broadcast_to([P, QC, VH, P])
                pool.tensor_tensor(gu[:, :, :].rearrange("p (c h) i -> p c h i", c=QC), gsl, mask, ALU.mult
                                   ).then_inc(s["gu_done"], 1)
                pool.wait_ge(s["nsq_done"], n + 1)
                pool.tensor_tensor(norm_k[:, :], nsq[:, :], tab["half"][:, 0:QC], ALU.pow).then_inc(s["norm_done"], 1)
                pool.wait_ge(s["prep_act"], 10 * n + 10 + 6)
                pool.tensor_tensor(zn[:, :, :, :].rearrange("p c h d -> p (c h) d"),
                                   zs[:, :, :, :].rearrange("p c h d -> p (c h) d"),
                                   tab["norm_w"].unsqueeze(1).broadcast_to([P, NM, DK]), ALU.mult
                                   ).then_inc(s["zn_done"], 1)
                for g in range(2):
                    pool.wait_ge(s["lraw_done"], 2 * n + g + 1)
                    for dst, mask in ((buf[g]["a"], "block"), (lm[g], "before")):
                        pool.tensor_tensor(dst[:, :, :], ln[g][:, :, :],
                                           tab[mask].unsqueeze(1).broadcast_to([P, GM, P]), ALU.mult
                                           ).then_inc(s["masked"], 1)
                    pool.wait_ge(s["masked"], 4 * n + 2 * g + 1)
                    pool.tensor_tensor(buf[g]["ya"][:, :, :], buf[g]["a"][:, :, :],
                                       c.ident[:, :].unsqueeze(1).broadcast_to([P, GM, P]), ALU.add
                                       ).then_inc(s["y1_done"], 1)
                for ch in range(QC):
                    m = QC * n + ch
                    pool.wait_ge(s["osc_link"], m + 1)
                    pool.tensor_tensor(osc[ch % 2][:, :], osc[ch % 2][:, :], tab["mhalf"][:, 0:VH], ALU.pow
                                       ).then_inc(s["osc_done"], 1)

            over_quads(pool, emit)

        @block.vector
        def _(dve):
            dve.memset(S[:, :, :], 0.0)
            dve.tensor_scalar(eye2[:, :], c.ident[:, :], 2.0, GRID, ALU.mult, ALU.subtract)
            dve.memset(raw[:, :, :], 0.0)
            dve.memset(c.Y[:, :, :], 0.0).then_inc(s["zeroed"], 1)
            dve.sem_inc(s["raw_free"], 1)
            dve.wait_ge(s["zeroed"], 1)

            def head(kh):
                dve.wait_ge(s["quad_done"], NQ * kh + 1)
                dve.wait_ge(s["w_landed"], 16 * (kh + 1))
                dve.tensor_copy(ws[:, :], landing[:, :]).then_inc(s["w_ready"], 1)
                dve.wait_ge(s["w_ready"], kh + 1)
                dve.sem_inc(s["w_taken"], 1)

            def emit(kh, q, n):
                for k in range(KCONV):
                    for m in range(CH):
                        if k == 0:
                            dve.wait_ge(s["prep_act"], 10 * n + 10 + m + 1)
                            ins = dve.tensor_scalar(cv[:, m, :], raw[:, m, 0:QT_], conv_w[:, m, 0:1], None, ALU.mult)
                        else:
                            dve.wait_ge(s["conv_step"], 16 * n + 4 * (k - 1) + m + 1)
                            ins = dve.scalar_tensor_tensor(cv[:, m, :], raw[:, m, k:k + QT_], conv_w[:, m, k:k + 1],
                                                           cv[:, m, :], ALU.mult, ALU.add)
                        ins.then_inc(s["conv_step"], 1)
                dve.wait_ge(s["conv_step"], 16 * n + 16)
                dve.sem_inc(s["raw_free"], 1)
                dve.wait_ge(s["sq_k"], 2 * n + 2)
                heads = ds(VH * kh, VH)
                tiles = ds(QC * q, QC)
                dve.tensor_scalar(nsq[:, :], sumsq[:, 0, :], EPS, None, ALU.add).then_inc(s["nsq_done"], 1)
                dve.tensor_scalar(qe[:, :], sumsq[:, 1, :], EPS, EPS * DK, ALU.add, ALU.mult)
                dve.tensor_copy(nd[:, :, :], tab["neg_decay"][:, tiles, heads])
                dve.tensor_copy(cd[:, :, :], tab["chunk_decay"][:, tiles, heads])
                dve.wait_ge(s["nsq_done"], n + 1)
                dve.reciprocal(rn[:, :], nsq[:, :]).then_inc(s["scal"], 1)
                dve.wait_ge(s["scal"], 3 * n + 1)
                dve.tensor_tensor(sn[:, :, :], tab["nbeta"][:, tiles, heads],
                                  rn[:, :].unsqueeze(2).broadcast_to([P, QC, VH]), ALU.mult).then_inc(s["scal"], 1)
                dve.wait_ge(s["scal"], 3 * n + 2)
                dve.tensor_tensor(snd[:, :, :], sn[:, :, :], tab["decay_after"][:, tiles, heads], ALU.mult
                                  ).then_inc(s["scal"], 1)
                dve.wait_ge(s["norm_done"], n + 1)
                for i in range(2):
                    dve.wait_ge(s["prep_mm"], 14 * n + 9 + i)
                    dve.tensor_tensor(vr[:, 2 * i:2 * i + 2, :, :],
                                      prep[i][:, :, :].rearrange("p (c h) d -> p c h d", c=2),
                                      norm_k[:, 2 * i:2 * i + 2].unsqueeze(2).unsqueeze(3).broadcast_to([P, 2, VH, DK]),
                                      ALU.mult).then_inc(s["prep_dve"], 1)
                for g in range(2):
                    dve.wait_ge(s["prep_act"], 10 * n + 10 + 9 + g)
                    dve.tensor_scalar(flat(gam[g][:, :, :]), flat(gam[g][:, :, :]), TINY, TINY, ALU.max,
                                      ALU.subtract).then_inc(s["flushed"], 1)
                    dve.wait_ge(s["flushed"], 2 * n + g + 1)
                    dve.wait_ge(s["prep_mm"], 14 * n + 13 + g)
                    bank = prep[g][:, :, :].rearrange("p (j x) d -> p j x d", x=2)
                    for j in range(2):
                        for h in range(VH):
                            last = dve.scalar_tensor_tensor(ln[g][:, VH * j + h, :], gam[g][:, VH * j + h, :],
                                                            sn[:, 2 * g + j, h:h + 1], bank[:, j, 0, :],
                                                            ALU.mult, ALU.mult)
                    last.then_inc(s["lraw_done"], 1)
                    dve.tensor_tensor(attn[g][:, :, :].rearrange("p (j h) d -> p j h d", j=2),
                                      gam[g][:, :, :].rearrange("p (j h) d -> p j h d", j=2),
                                      bank[:, :, 1, :].unsqueeze(2).broadcast_to([P, 2, VH, P]), ALU.mult
                                      ).then_inc(s["prep_dve"], 1)

                def unit(g, u):
                    name, B = UNITS[u], buf[g]
                    if name not in BY_DVE:
                        return
                    dve.wait_ge(s[f"inv_mm{g}"], NU * n + u + 1)
                    out, bank = B[OUT[name]][:, :, :], inv[g][u % 2][:, :, :]
                    eye = c.ident[:, :].unsqueeze(1).broadcast_to([P, GM, P])
                    if name == "im":
                        ins = dve.tensor_tensor(out, bank, eye, ALU.subtract)
                    elif name in ("y2", "y3", "y4"):
                        old = {"y2": "ya", "y3": "yb", "y4": "ya"}[name]
                        if name == "y2":
                            dve.wait_ge(s["y1_done"], 2 * n + g + 1)
                        else:
                            copied(dve, g, [{"y3": "y2", "y4": "y3"}[name]], n)
                        ins = dve.tensor_tensor(out, B[old][:, :, :], bank, ALU.add)
                        if name == "y4":
                            ins.then_inc(s["y4_sum"], 1)
                            dve.wait_ge(s["y4_sum"], 2 * n + g + 1)
                            ins = dve.tensor_scalar(out, out, GRID, GRID, ALU.add, ALU.subtract)
                    elif name[0] == "r":
                        ins = dve.scalar_tensor_tensor(out, bank, GRID,
                                                       eye2[:, :].unsqueeze(1).broadcast_to([P, GM, P]),
                                                       ALU.add, ALU.add)
                    else:
                        ins = dve.tensor_scalar(out, bank, GRID, GRID, ALU.add, ALU.subtract)
                    ins.then_inc(s[f"inv_dve{g}"], 1)

                for u in range(NU):
                    for g in range(2):
                        unit(g, u)

                def both(ap):
                    return ap.unsqueeze(2).broadcast_to([P, VH, DK])

                def output(ch):
                    m = QC * n + ch
                    dve.wait_ge(s["osc_done"], m + 1)
                    dve.wait_ge(s["zn_done"], n + 2)
                    for h in range(VH):
                        last = dve.scalar_tensor_tensor(gated[ch % 2][:, h, :], on[ch % 2][:, h, :],
                                                        osc[ch % 2][:, h:h + 1], zn[:, ch, h, :], ALU.mult, ALU.mult)
                    last.then_inc(s["gated_done"], 1)
                    dve.wait_ge(s["y_done"], m + 1)
                    y = c.Y[:, ds(QC * q + ch, 1), :].rearrange("p a d -> p (a d)")
                    dve.tensor_tensor(y, y, flat(prep[1][:, 0:2, :]), ALU.add).then_inc(s["y_added"], 1)

                for ch in range(QC):
                    m = QC * n + ch
                    dve.wait_ge(s["ks_done"], m + 1)
                    for h in range(VH):
                        last = dve.scalar_tensor_tensor(r0[:, h, :], ra[:, 0, h, :], nd[:, ch, h:h + 1],
                                                        vr[:, ch, h, :], ALU.mult, ALU.add)
                    last.then_inc(s["r_done"], 1)
                    dve.wait_ge(s["u_done"], m + 1)
                    dve.tensor_tensor(v3[:, :, :], rb[:, 0, :, :], both(snd[:, ch, :]), ALU.mult
                                      ).then_inc(s["v3_done"], 1)
                    dve.tensor_tensor(v2[:, :, :], rb[:, 0, :, :], both(sn[:, ch, :]), ALU.mult
                                      ).then_inc(s["v2_done"], 1)
                    dve.wait_ge(s["sv_done"], m + 1)
                    for h in range(VH):
                        last = dve.scalar_tensor_tensor(S[:, h, :], S[:, h, :], cd[:, ch, h:h + 1], ra[:, 0, h, :],
                                                        ALU.mult, ALU.subtract)
                    last.then_inc(s["s_done"], 1)
                    dve.wait_ge(s["av_done"], m + 1)
                    dve.tensor_tensor(on[ch % 2][:, :, :], tq[ch % 2][:, :, :], rb[:, 1, :, :], ALU.add
                                      ).then_inc(s["o_done"], 1)
                    if ch:
                        output(ch - 1)
                output(QC - 1)
                dve.sem_inc(s["quad_done"], 1)

            over_quads(dve, emit, head)


def program(nc, a, out, only=None, upto=None):
    with ExitStack() as ctx:
        c = Core(nc, ctx)
        setup(c, a["x"])
        if only in (None, "attn"):
            norm_phase(c, "ln0", add_branch=False)
            with ExitStack() as attn:
                QT = c.sb(attn, "q_t", [P, HEADS, T], BF16)
                KT = c.sb(attn, "k_t", [P, HEADS, T], BF16)
                V = c.sb(attn, "v", [P, NT, HEADS, DH], F32)
                qkv_phase(c, QT, KT, V, a["wqkv"], a["bqkv"], a["rope"])
                attention_phase(c, QT, KT, V)
            turn_phase(c, "ao")
            projection_phase(c, a["out_w"], a["out_b"])
            if upto == "attn":
                norm_phase(c, "ln1", True, want_t=False, out_dram=out)
                return
            norm_phase(c, "ln1", True)
        elif only == "moe":
            norm_phase(c, "ln1", False)
        if only in (None, "moe"):
            with ExitStack() as moe:
                combine = c.sb(moe, "combine", [P, NT, ALL_EXPERTS], F32)
                router_phase(c, combine, a["gate_w"])
                moe_phase(c, combine, a["wgu"], a["wdn"])
            if only == "moe":
                norm_phase(c, "ln2", True, want_t=False, out_dram=out)
                return
            norm_phase(c, "ln2", True)
        elif only == "gdn":
            norm_phase(c, "ln2", False)
        if only in (None, "gdn"):
            delta_phase(c, a)
            if only == "gdn":
                norm_phase(c, "ln3", True, want_t=False, out_dram=out)
                return
            norm_phase(c, "ln3", True)
        else:
            norm_phase(c, "ln3", False)
        ffn_phase(c, a["ffn_g"], a["ffn_u"], a["ffn_d"], a["ffn_gs"], a["ffn_us"], a["ffn_ds"])
        norm_phase(c, "ln4", True, want_t=False, out_dram=out)


def layout(inputs):
    import numpy as np

    def rows(w, parts):
        return np.ascontiguousarray(w.reshape(parts, P, -1).transpose(1, 0, 2))

    g = {k: np.asarray(v) for k, v in inputs.items()}
    out = {"x": g["L0_attn_x"].reshape(T, D)}
    out["wqkv"] = rows(np.concatenate([g[f"L0_attn_{n}_w"].T for n in "qkv"], 1), KD)
    out["bqkv"] = np.concatenate([g[f"L0_attn_{n}_b"] for n in "qkv"])[None]
    out["out_w"] = rows(g["L0_attn_out_w"].T, KD)
    out["out_b"] = g["L0_attn_out_b"][None]
    inv = (1.0 / np.float32(10000.0) ** (np.arange(0, DH, 2, dtype=np.float32) / np.float32(DH))).astype(np.float32)
    angle = np.arange(T, dtype=np.float32)[:, None] * inv[None]
    cos, sin = np.cos(angle), np.sin(angle)
    table = np.stack([np.concatenate([cos, cos], 1), np.concatenate([-sin, sin], 1)], 1).astype(np.float32)
    out["rope"] = np.ascontiguousarray(table.reshape(NT, P, 2, DH).transpose(1, 0, 2, 3))
    out["gate_w"] = rows(g["L0_ffn_gate_w"].T, KD)
    shared = g["L0_ffn_shared_gate_up"].reshape(D, 2, SHARED_PARTS, INTER).transpose(2, 0, 1, 3)
    wgu = np.concatenate([g["L0_ffn_w_gate_up"], shared.reshape(SHARED_PARTS, D, 2 * INTER)])
    out["wgu"] = np.ascontiguousarray(wgu.reshape(ALL_EXPERTS, KD, P, 2 * INTER).transpose(2, 1, 0, 3))
    pad = np.zeros((HT * P - HCAT, D), np.float32)
    out["wdn"] = rows(np.concatenate([g["L0_ffn_w_down"].reshape(-1, D), g["L0_ffn_shared_down"], pad]), HT)
    kd = HK * DK
    w_qkv, w_z = g["L1_attn_w_qkv"], g["L1_attn_w_z"]
    conv, w_o = g["L1_attn_conv_w"], g["L1_attn_w_out"]
    heads = []
    for h in range(HK):
        cols = [slice(h * DK, (h + 1) * DK), slice(kd + h * DK, kd + (h + 1) * DK)]
        cols += [slice(2 * kd + (VH * h + j) * DK, 2 * kd + (VH * h + j + 1) * DK) for j in range(VH)]
        zcols = slice(VH * h * DK, VH * (h + 1) * DK)
        w = rows(np.concatenate([w_qkv[:, x] for x in cols] + [w_z[:, zcols]], 1), KD).reshape(P, -1)
        taps = np.stack([conv[:, x].T for x in cols], 1).reshape(P, -1)
        heads.append(np.concatenate([w, taps, rows(w_o[zcols], VH).reshape(P, -1)], 1))
    out["w_delta"] = np.stack(heads)
    out["w_ab"] = rows(np.concatenate([g["L1_attn_w_b"], g["L1_attn_w_a"]], 1), KD)
    out["dt_bias"] = g["L1_attn_dt_bias"][None]
    out["a_log"] = g["L1_attn_A_log"][None]
    out["norm_w"] = g["L1_attn_norm_w"][None]
    out["ffn_g"] = rows(g["L1_ffn_gate_w"].T, KD).reshape(P, -1)
    out["ffn_u"] = rows(g["L1_ffn_up_w"].T, KD).reshape(P, -1)
    out["ffn_d"] = rows(g["L1_ffn_down_w"].T, FT).reshape(P, -1)
    out["ffn_gs"] = np.ascontiguousarray(g["L1_ffn_gate_scale"].reshape(FT, P).T)
    out["ffn_us"] = np.ascontiguousarray(g["L1_ffn_up_scale"].reshape(FT, P).T)
    out["ffn_ds"] = g["L1_ffn_down_scale"][None]
    return out


def kernel(**inputs):
    import concourse.bacc as _bacc
    from concourse.bass_utils import run_bass_kernel_spmd as _run

    nc = _bacc.Bacc("TRN2", target_bir_lowering=False, num_devices=1)
    arrays, aps = {}, {}
    for name, arr in layout(inputs).items():
        arrays[f"in_{name}"] = arr
        aps[name] = nc.dram_tensor(f"in_{name}", arr.shape, mybir.dt.from_np(arr.dtype), kind="ExternalInput").ap()
    out = nc.dram_tensor("out_0", (T, D), F32, kind="ExternalOutput").ap()
    program(nc, aps, out)
    r = _run(nc, [arrays], core_ids=[0])
    return r.results[0]["out_0"].reshape(1, T, D)
```

```python
from contextlib import ExitStack

import concourse.bass as bass
from concourse import mybir

F32 = mybir.dt.float32
BF16 = mybir.dt.bfloat16
U32 = mybir.dt.uint32
I32 = mybir.dt.int32
ALU = mybir.AluOpType
ACT = mybir.ActivationFunctionType
AX = mybir.AxisListType
ds = bass.ds

P = 128
T = 2048
D = 256
NT = T // P
KD = D // P
LN_EPS = 1e-5

HEADS, DH = 16, 16
PARTS = 6
SPLIT_ROWS = PARTS * DH
MAX_ROWS = 3
SCORE_ROWS = SPLIT_ROWS + MAX_ROWS

EXPERTS, INTER = 16, 176
SHARED_PARTS = 2
ALL_EXPERTS = EXPERTS + SHARED_PARTS
HCAT = ALL_EXPERTS * INTER
HT = -(-HCAT // P)

FFN = 1024
FT = FFN // P


def flat(ap):
    names = "abcde"[: len(ap.shape) - 1]
    return ap.rearrange(f"p {' '.join(names)} -> p ({' '.join(names)})")


class Core:

    def __init__(self, nc, ctx):
        self.nc, self.ctx, self.n = nc, ctx, 0
        self.X = self.sb(ctx, "residual", [P, NT, D], F32)
        self.XT = self.sb(ctx, "normed_t", [P, KD, T], F32)
        self.Y = self.sb(ctx, "branch", [P, NT, D], F32)
        self.ident = self.sb(ctx, "ident", [P, P], F32)
        self.identb = self.sb(ctx, "identb", [P, P], BF16)
        self.ones = self.sb(ctx, "ones_row", [1, P], F32)

    def sb(self, ctx, name, shape, dt):
        return ctx.enter_context(self.nc.sbuf_tensor(name, shape, dt))

    def ps(self, ctx, name, shape, dt=F32):
        return ctx.enter_context(self.nc.psum_tensor(name, shape, dt))

    def sem(self, ctx, name):
        return ctx.enter_context(self.nc.semaphore(name))


def setup(c, x_dram):
    nc = c.nc
    with ExitStack() as ctx:
        x_in = c.sem(ctx, "x_in")
        ident0 = c.sem(ctx, "ident_zeroed")
        ident1 = c.sem(ctx, "ident_made")
        block = ctx.enter_context(nc.Block())

        @block.sync
        def _(sp):
            sp.dma_start(c.X[:, :, :], x_dram.rearrange("(t p) d -> p t d", p=P)).then_inc(x_in, 16)
            sp.wait_ge(x_in, 16)

        @block.gpsimd
        def _(pool):
            pool.memset(c.ident[:, :], 0.0).then_inc(ident0, 1)
            pool.memset(c.ones[:, :], 1.0)
            pool.wait_ge(ident0, 1)
            pool.affine_select(out=c.ident[:, :], in_=c.ident[:, :], compare_op=ALU.not_equal, fill=1.0,
                               base=0, pattern=[[-1, P]], channel_multiplier=1).then_inc(ident1, 1)
            pool.wait_ge(ident1, 1)
            pool.tensor_copy(c.identb[:, :], c.ident[:, :])


def norm_phase(c, tag, add_branch, want_t=True, out_dram=None):
    nc = c.nc
    rounds = (1 if add_branch else 0) + (1 if want_t else 0)
    with ExitStack() as ctx:
        normed = c.sb(ctx, f"{tag}_normed", [P, NT, D], F32)
        stats = c.sb(ctx, f"{tag}_stats", [P, NT, 6], F32)
        mv = c.sb(ctx, f"{tag}_mean_var", [P, NT, 2], F32)
        rstd = c.sb(ctx, f"{tag}_rstd", [P, NT], F32)
        mhalf = c.sb(ctx, f"{tag}_minus_half", [P, NT], F32)
        tp = [c.ps(ctx, f"{tag}_tp{i}", [P, 2, KD, P]) for i in range(2)]
        stats_done = c.sem(ctx, f"{tag}_stats_done")
        var_done = c.sem(ctx, f"{tag}_var_done")
        rstd_done = c.sem(ctx, f"{tag}_rstd_done")
        scaled = c.sem(ctx, f"{tag}_scaled")
        added = c.sem(ctx, f"{tag}_added") if add_branch else None
        turned = c.sem(ctx, f"{tag}_turned") if want_t else None
        copied = c.sem(ctx, f"{tag}_copied") if want_t else None
        stored = c.sem(ctx, f"{tag}_stored") if out_dram is not None else None
        block = ctx.enter_context(nc.Block())

        @block.vector
        def _(dve):
            def normalise(src, r):
                with dve.Fori(0, NT) as t:
                    dve.bn_stats(stats[:, ds(t, 1), :].rearrange("p a s -> p (a s)"),
                                 src[:, ds(t, 1), :].rearrange("p a s -> p (a s)")).then_inc(stats_done, 1)
                dve.wait_ge(stats_done, (NT + 1) * r + NT)
                for t in range(NT):
                    last = dve.bn_aggr(mv[:, t, :], stats[:, t, :])
                last.then_inc(stats_done, 1)
                dve.wait_ge(rstd_done, 2 * (r + 1))
                with dve.Fori(0, NT) as t:
                    dve.tensor_scalar(normed[:, ds(t, 1), :].rearrange("p a s -> p (a s)"),
                                      src[:, ds(t, 1), :].rearrange("p a s -> p (a s)"),
                                      mv[:, ds(t, 1), 0:1].rearrange("p a s -> p (a s)"), rstd[:, ds(t, 1)],
                                      ALU.subtract, ALU.mult).then_inc(scaled, 1)

            if add_branch:
                normalise(c.Y, 0)
                dve.wait_ge(scaled, NT)
                dve.tensor_tensor(flat(c.X[:, :, :]), flat(c.X[:, :, :]), flat(normed[:, :, :]),
                                  ALU.add).then_inc(added, 1)
                dve.wait_ge(added, 1)
            if want_t:
                normalise(c.X, rounds - 1)

        @block.gpsimd
        def _(pool):
            pool.memset(mhalf[:, :], -0.5).then_inc(var_done, 1)
            for r in range(rounds):
                pool.wait_ge(stats_done, (NT + 1) * (r + 1))
                pool.tensor_scalar(rstd[:, :], mv[:, :, 1], LN_EPS, None, ALU.add).then_inc(rstd_done, 1)
                pool.wait_ge(rstd_done, 2 * r + 1)
                pool.wait_ge(var_done, 1)
                pool.tensor_tensor(rstd[:, :], rstd[:, :], mhalf[:, :], ALU.pow).then_inc(rstd_done, 1)

        if want_t:
            transpose_tiles(c, block, normed, c.XT, tp, scaled, NT * (rounds - 1), turned, copied)

        if out_dram is not None:
            @block.sync
            def _(sp):
                sp.wait_ge(added, 1)
                sp.dma_start(out_dram.rearrange("(t p) d -> p t d", p=P), c.X[:, :, :]).then_inc(stored, 16)
                sp.wait_ge(stored, 16)


def transpose_tiles(c, block, src, dst, tp, ready, ready_base, turned, copied):

    @block.tensor
    def _(pe):
        for i in range(NT // 2):
            if ready is not None:
                pe.wait_ge(ready, ready_base + 2 * i + 2)
            if i >= 2:
                pe.wait_ge(copied, i - 1)
            for j in range(2):
                for k in range(KD):
                    last = pe.transpose(tp[i % 2][:, j, k, :], src[:, 2 * i + j, k * P:(k + 1) * P],
                                        c.ident[:, :])
            last.then_inc(turned, 1)

    @block.scalar
    def _(act):
        for i in range(NT // 2):
            act.wait_ge(turned, i + 1)
            out = dst[:, :, 2 * i * P:(2 * i + 2) * P].rearrange("p k (j c) -> p j k c", j=2)
            act.activation(out, tp[i % 2][:, :, :, :], ACT.Copy).then_inc(copied, 1)


def qkv_phase(c, QT, KT, V, w_dram, bias_dram, rope_dram):
    nc = c.nc
    with ExitStack() as ctx:
        W = flat(c.Y[:, 0:6, :]).rearrange("p (k n) -> p k n", k=KD)
        bias = c.sb(ctx, "qkv_bias", [1, 3 * D], F32)
        rope = c.sb(ctx, "rope", [P, NT, 2, DH], F32)
        xs = [c.Y[:, 6 + j, :].rearrange("p (k n) -> p k n", k=KD) for j in range(2)]
        QK = 2 * HEADS
        cosp = flat(c.Y[:, 8:10, :]).rearrange("p (h d) -> p h d", h=QK)
        rot = flat(c.Y[:, 10:12, :]).rearrange("p (h d) -> p h d", h=QK)
        rest = flat(c.Y[:, 12:14, :]).rearrange("p (h d) -> p h d", h=QK)
        hi, mid = (c.Y[:, 14 + j, :].bitcast(BF16).rearrange("p (h d) -> p h d", h=QK) for j in range(2))
        lo = c.sb(ctx, "lo", [P, QK, DH], BF16)
        stack = [c.sb(ctx, f"stack{i}", [P, HEADS, PARTS, DH], BF16) for i in range(2)]
        qk_ps = [c.ps(ctx, f"qk_ps{j}", [P, QK, DH]) for j in range(2)]
        v_ps = [c.ps(ctx, f"v_ps{j}", [P, 512]) for j in range(2)]
        tp = [c.ps(ctx, f"stack_tp{i}", [P, 8, P], BF16) for i in range(4)]
        loaded = c.sem(ctx, "qkv_loaded")
        xs_free = c.sem(ctx, "xs_free")
        xs_ready = c.sem(ctx, "xs_ready")
        qkv_free = c.sem(ctx, "qkv_free")
        qkv_done = c.sem(ctx, "qkv_done")
        rope_step = c.sem(ctx, "rope_step")
        hi_done = c.sem(ctx, "hi_done")
        rest_done = c.sem(ctx, "rest_done")
        mid_done = c.sem(ctx, "mid_done")
        lo_done = c.sem(ctx, "lo_done")
        q_stacked = c.sem(ctx, "q_stacked")
        k_stacked = c.sem(ctx, "k_stacked")
        tp_done = c.sem(ctx, "stack_tp_done")
        tp_copied = c.sem(ctx, "stack_tp_copied")
        block = ctx.enter_context(nc.Block())

        @block.sync
        def _(sp):
            sp.dma_start(W, w_dram).then_inc(loaded, 16)
            sp.dma_start(bias[:, :], bias_dram).then_inc(loaded, 16)
            sp.dma_start(rope[:, :, :, :], rope_dram).then_inc(loaded, 16)

        @block.gpsimd
        def _(pool):
            with pool.Fori(0, NT // 2) as i:
                for j in range(2):
                    t = 2 * i + j
                    pool.wait_ge(xs_free, t + 1)
                    pool.tensor_copy(xs[j], c.XT[:, :, ds(t * P, P)]).then_inc(xs_ready, 1)

        @block.tensor
        def _(pe):
            pe.sem_inc(xs_free, 2)
            pe.sem_inc(tp_done, 4)
            pe.wait_ge(loaded, 48)
            with pe.Fori(0, NT // 2) as i:
                for j in range(2):
                    t = 2 * i + j
                    pe.wait_ge(xs_ready, t + 1)
                    pe.wait_ge(qkv_free, t + 1)
                    for out, lo_, n in ((flat(qk_ps[j][:, :, :]), 0, 2 * D), (v_ps[j][:, 0:D], 2 * D, D)):
                        for k in range(KD):
                            pe.matmul(out, xs[j][:, k, :], W[:, k, lo_:lo_ + n], start=(k == 0), stop=False)
                        last = pe.matmul(out, c.ones[:, :], bias[:, lo_:lo_ + n], start=False, stop=True)
                    last.then_inc(qkv_done, 1)
                    for s, stacked in ((0, q_stacked), (1, k_stacked)):
                        pe.wait_ge(stacked, t + 1)
                        for half in range(2):
                            pe.wait_ge(tp_copied, 4 * t + 2 * s + half + 1)
                            for h in range(8):
                                last = pe.transpose(tp[2 * s + half][0:SPLIT_ROWS, h, :],
                                                    stack[s][:, 8 * half + h, :, :].rearrange("p a b -> p (a b)"),
                                                    c.identb[:, :])
                            last.then_inc(tp_done, 1)

        @block.scalar
        def _(act):
            act.sem_inc(tp_copied, 4)
            with act.Fori(0, NT // 2) as i:
                for j in range(2):
                    t = 2 * i + j
                    act.wait_ge(qkv_done, t + 1)
                    act.activation(V[:, ds(t, 1), :, :].rearrange("p a h d -> p (a h d)"), v_ps[j][:, 0:D],
                                   ACT.Copy).then_inc(xs_free, 1)
                    act.wait_ge(rest_done, 2 * t + 1)
                    act.activation(flat(hi), flat(rest), ACT.Copy).then_inc(hi_done, 1)
                    act.wait_ge(rest_done, 2 * t + 2)
                    act.activation(flat(mid), flat(rest), ACT.Copy).then_inc(mid_done, 1)
                    act.wait_ge(lo_done, t + 1)
                    act.wait_ge(tp_done, 4 * t + 4)
                    for part, src in ((0, hi), (3, hi), (5, hi), (1, mid), (4, mid), (2, lo)):
                        last = act.activation(stack[1][:, :, part, :], src[:, HEADS:QK, :], ACT.Copy)
                    last.then_inc(k_stacked, 1)
                    for s, dst in ((0, QT), (1, KT)):
                        for half in range(2):
                            act.wait_ge(tp_done, 4 * t + 2 * s + half + 1 + 4)
                            act.activation(dst[0:SPLIT_ROWS, 8 * half:8 * half + 8, ds(t * P, P)],
                                           tp[2 * s + half][0:SPLIT_ROWS, :, :], ACT.Copy).then_inc(tp_copied, 1)

        @block.vector
        def _(dve):
            dve.sem_inc(qkv_free, 2)
            half = DH // 2
            dve.memset(KT[SPLIT_ROWS:SCORE_ROWS, :, :], 1.0)
            dve.wait_ge(loaded, 48)
            with dve.Fori(0, NT // 2) as i:
                for j in range(2):
                    t = 2 * i + j
                    src = qk_ps[j]

                    def table(k, a, n):
                        return rope[:, ds(t, 1), k, a:a + n].broadcast_to([P, QK, n])

                    dve.wait_ge(qkv_done, t + 1)
                    dve.tensor_tensor(cosp, src[:, :, :], table(0, 0, DH), ALU.mult)
                    dve.tensor_tensor(rot[:, :, 0:half], src[:, :, half:DH], table(1, 0, half), ALU.mult)
                    dve.tensor_tensor(rot[:, :, half:DH], src[:, :, 0:half], table(1, half, half),
                                      ALU.mult).then_inc(qkv_free, 1)
                    dve.wait_ge(qkv_free, t + 3)
                    dve.tensor_tensor(rest, cosp, rot, ALU.add).then_inc(rest_done, 1)
                    dve.wait_ge(hi_done, t + 1)
                    dve.tensor_tensor(rest, rest, hi, ALU.subtract).then_inc(rest_done, 1)
                    dve.wait_ge(mid_done, t + 1)
                    dve.tensor_tensor(lo[:, :, :], rest, mid, ALU.subtract).then_inc(lo_done, 1)
                    dve.wait_ge(lo_done, t + 1)
                    dve.wait_ge(tp_done, 4 * t + 2)
                    for part, s in ((0, hi), (1, hi), (2, hi), (3, mid), (4, mid), (5, lo)):
                        last = dve.tensor_copy(stack[0][:, :, part, :], s[:, 0:HEADS, :])
                    last.then_inc(q_stacked, 1)
                    dve.wait_ge(k_stacked, t + 1)


def attention_phase(c, QT, KT, V):
    nc = c.nc
    QB = 4
    BQ = T // QB
    with ExitStack() as ctx:
        probs = c.XT
        vs = c.sb(ctx, "v_staged", [P, NT, 32], F32)
        part_max = c.sb(ctx, "part_max", [P, NT, 4], F32)
        neg_max = c.sb(ctx, "neg_max", [P, NT], F32)
        max_parts = c.sb(ctx, "max_parts", [P, MAX_ROWS + 2, NT], BF16)
        PAD = (MAX_ROWS + 2) * NT
        max_t = c.sb(ctx, "max_t", [MAX_ROWS * NT, P], BF16)
        out_sb = c.sb(ctx, "out_sb", [P, BQ], F32)
        rden = c.sb(ctx, "rden", [P, NT], F32)
        mx = [c.ps(ctx, f"mx{i}", [P, 512]) for i in range(2)]
        sc = [c.ps(ctx, f"sc{i}", [P, 2, 512]) for i in range(2)]
        o_ps = c.ps(ctx, "o_ps", [P, 512])
        tr_ps = c.ps(ctx, "tr_ps", [P, 512])
        s = {n: c.sem(ctx, n) for n in (
            "pad_set", "v_staged_sem", "mx_done", "mx_free", "sc_done", "exp_done", "pv_done", "max_step",
            "parts_ready", "max_turned", "max_copied", "rows_in", "o_copied", "o_turned", "rden_done", "o_free")}
        block = ctx.enter_context(nc.Block())

        def program(engine, emit):
            with engine.Fori(0, 2) as i:
                emit(i, True, False)
            with engine.Fori(2, HEADS) as i:
                emit(i, True, True)
            with engine.Fori(HEADS, HEADS + 2) as i:
                emit(i, False, True)

        @block.gpsimd
        def _(pool):
            pool.memset(vs[:, :, DH:32], 0.0).then_inc(s["pad_set"], 1)
            pool.wait_ge(s["pad_set"], 1)
            pool.memset(vs[:, :, DH:DH + 1], 1.0).then_inc(s["pad_set"], 1)
            pool.wait_ge(s["pad_set"], 2)

            with pool.Fori(0, HEADS) as h:
                for kt in range(NT):
                    pool.wait_ge(s["pv_done"], NT * h + kt + 1)
                    pool.tensor_copy(vs[:, kt, 0:DH], V[:, kt, ds(h, 1), :].rearrange("p a d -> p (a d)")
                                     ).then_inc(s["v_staged_sem"], 1)

        @block.tensor
        def _(pe):
            pe.sem_inc(s["mx_free"], 2)
            pe.sem_inc(s["pv_done"], NT)
            pe.sem_inc(s["max_turned"], 1)

            def emit(i, do_max, do_exp):
                h = i - 2

                def q_cols(head, a, n, rows=SCORE_ROWS):
                    return QT[0:rows, ds(head, 1), a:a + n].rearrange("p a b -> p (a b)")

                def k_cols(head, a, n, rows=SCORE_ROWS):
                    return KT[0:rows, ds(head, 1), a:a + n].rearrange("p a b -> p (a b)")

                def scores(kt, u):
                    pe.wait_ge(s["exp_done"], 2 * NT * h + 2 * kt + u + 1)
                    for b in range(2):
                        last = pe.matmul(sc[u][:, b, :], k_cols(h, kt * P, P), q_cols(h, (2 * u + b) * BQ, BQ),
                                         start=True, stop=True)
                    last.then_inc(s["sc_done"], 1)

                def maxima(qt, u):
                    for b in (2 * u, 2 * u + 1):
                        pe.wait_ge(s["mx_free"], 4 * NT * i + 4 * qt + b + 1)
                        pe.matmul(mx[b % 2][:, :], q_cols(i, qt * P, P, SPLIT_ROWS),
                                  k_cols(i, b * 512, 512, SPLIT_ROWS), start=True, stop=True
                                  ).then_inc(s["mx_done"], 1)

                def weigh(kt):
                    pe.wait_ge(s["exp_done"], 2 * NT * h + 2 * kt + 2 + 2)
                    pe.wait_ge(s["v_staged_sem"], NT * h + kt + 1)
                    if kt == 0:
                        pe.wait_ge(s["o_free"], h + 1)
                    for qb in range(QB):
                        last = pe.matmul(o_ps[32 * qb:32 * qb + 32, :], vs[:, kt, :],
                                         probs[:, kt % 2, qb * BQ:(qb + 1) * BQ], start=(kt == 0),
                                         stop=(kt == NT - 1))
                    last.then_inc(s["pv_done"], 1)

                if do_exp:
                    pe.wait_ge(s["rows_in"], 16 * MAX_ROWS * (h + 2))
                for kt in range(NT):
                    for u in range(2):
                        if do_exp:
                            scores(kt, u)
                        if do_max:
                            maxima(kt, u)
                    if do_exp and kt:
                        weigh(kt - 1)
                if do_exp:
                    weigh(NT - 1)
                if do_max:
                    pe.wait_ge(s["max_copied"], i + 1)
                    pe.wait_ge(s["parts_ready"], i + 1)
                    pe.transpose(tr_ps[0:PAD, 0:P // 2].bitcast(BF16),
                                 max_parts[:, :, :].rearrange("p a b -> p (a b)"), c.identb[:, :]
                                 ).then_inc(s["max_turned"], 1)
                if do_exp:
                    pe.wait_ge(s["o_copied"], h + 1)
                    for j in range(QB):
                        last = pe.transpose(o_ps[:, j * P:(j + 1) * P], out_sb[:, j * P:(j + 1) * P],
                                            c.ident[:, :])
                    last.then_inc(s["o_turned"], 1)

            program(pe, emit)

        @block.scalar
        def _(act):
            act.sem_inc(s["exp_done"], 2)
            act.sem_inc(s["max_copied"], 1)

            def emit(i, do_max, do_exp):
                h = i - 2
                if do_exp:
                    for kt in range(NT):
                        for u in range(2):
                            act.wait_ge(s["sc_done"], 2 * NT * h + 2 * kt + u + 1)
                            if u == 0:
                                act.wait_ge(s["pv_done"], NT * h + kt + NT - 1)
                            act.activation(probs[:, kt % 2, u * 2 * BQ:(u + 1) * 2 * BQ], flat(sc[u][:, :, :]),
                                           ACT.Exp, scale=float(DH) ** -0.5).then_inc(s["exp_done"], 1)
                    act.wait_ge(s["pv_done"], NT * h + NT + NT)
                    act.activation(out_sb[:, :], o_ps[:, :], ACT.Copy).then_inc(s["o_copied"], 1)
                if do_max:
                    act.wait_ge(s["max_turned"], i + 2)
                    act.wait_ge(s["rows_in"], 16 * MAX_ROWS * (i + 1))
                    act.activation(max_t[:, :], tr_ps[0:MAX_ROWS * NT, 0:P // 2].bitcast(BF16), ACT.Copy
                                   ).then_inc(s["max_copied"], 1)

            program(act, emit)

        @block.sync
        def _(sp):
            sp.sem_inc(s["rows_in"], 16 * MAX_ROWS)
            with sp.Fori(0, HEADS) as h:
                sp.wait_ge(s["max_copied"], h + 2)
                for part in range(MAX_ROWS):
                    row = SPLIT_ROWS + part
                    dst = QT[row:row + 1, ds(h, 1), :].rearrange("r a (t c) -> r (a t) c", t=NT)
                    sp.dma_start(dst, max_t[part * NT:(part + 1) * NT, :]).then_inc(s["rows_in"], 16)

        @block.vector
        def _(dve):
            dve.sem_inc(s["o_free"], 1)
            dve.memset(max_parts[:, MAX_ROWS:, :], 0.0)

            def emit(i, do_max, do_exp):
                h = i - 2
                links = 2 * MAX_ROWS - 1

                def chained(ins, n):
                    ins.then_inc(s["max_step"], 1)
                    dve.wait_ge(s["max_step"], links * i + n)

                if do_max:
                    for qt in range(NT):
                        for b in range(4):
                            dve.wait_ge(s["mx_done"], 4 * NT * i + 4 * qt + b + 1)
                            dve.reduce_max(part_max[:, qt, b:b + 1], mx[b % 2][:, :], AX.X
                                           ).then_inc(s["mx_free"], 1)
                    dve.wait_ge(s["mx_free"], 4 * NT * i + 4 * NT + 2)
                    chained(dve.tensor_reduce(neg_max[:, :], part_max[:, :, :], AX.X, ALU.max, negate=True), 1)
                    dve.wait_ge(s["max_turned"], i + 1)
                    for part in range(MAX_ROWS - 1):
                        chained(dve.tensor_copy(max_parts[:, part, :], neg_max[:, :]), 2 * part + 2)
                        chained(dve.tensor_tensor(neg_max[:, :], neg_max[:, :], max_parts[:, part, :],
                                                  ALU.subtract), 2 * part + 3)
                    dve.tensor_copy(max_parts[:, MAX_ROWS - 1, :], neg_max[:, :]).then_inc(s["parts_ready"], 1)
                if do_exp:
                    dve.wait_ge(s["o_turned"], h + 1)
                    o = o_ps[:, :].rearrange("p (j b e) -> p b j e", j=QB, b=QB)
                    r = rden[:, :].rearrange("p (b j) -> p b j", b=QB)
                    dve.reciprocal(r, o[:, :, :, DH]).then_inc(s["rden_done"], 1)
                    dve.wait_ge(s["rden_done"], h + 1)
                    y = c.Y[:, :, ds(h * DH, DH)].rearrange("p (b j) d -> p b j d", b=QB)
                    dve.tensor_tensor(y, o_ps[:, :].rearrange("p (j b e) -> p b j e", j=QB, b=QB)[:, :, :, 0:DH],
                                      r.unsqueeze(3).broadcast_to([P, QB, QB, DH]), ALU.mult
                                      ).then_inc(s["o_free"], 1)

            program(dve, emit)


def projection_phase(c, w_dram, bias_dram):
    nc = c.nc
    with ExitStack() as ctx:
        W = c.sb(ctx, "out_w", [P, KD, D], F32)
        bias = c.sb(ctx, "out_bias", [1, D], F32)
        ps = [c.ps(ctx, f"proj_ps{i}", [P, 512]) for i in range(2)]
        loaded = c.sem(ctx, "out_w_loaded")
        done = c.sem(ctx, "proj_done")
        copied = c.sem(ctx, "proj_copied")
        block = ctx.enter_context(nc.Block())

        @block.sync
        def _(sp):
            sp.dma_start(W[:, :, :], w_dram).then_inc(loaded, 16)
            sp.dma_start(bias[:, :], bias_dram).then_inc(loaded, 16)

        @block.tensor
        def _(pe):
            pe.wait_ge(loaded, 32)
            for t in range(NT):
                if t >= 2:
                    pe.wait_ge(copied, t - 1)
                for k in range(KD):
                    pe.matmul(ps[t % 2][:, 0:D], c.XT[:, k, t * P:(t + 1) * P], W[:, k, :], start=(k == 0),
                              stop=False)
                pe.matmul(ps[t % 2][:, 0:D], c.ones[:, :], bias[:, :], start=False, stop=True).then_inc(done, 1)

        @block.scalar
        def _(act):
            for t in range(NT):
                act.wait_ge(done, t + 1)
                act.activation(c.Y[:, t, :], ps[t % 2][:, 0:D], ACT.Copy).then_inc(copied, 1)


def turn_phase(c, tag):
    with ExitStack() as ctx:
        tp = [c.ps(ctx, f"{tag}_tp{i}", [P, 2, KD, P]) for i in range(2)]
        turned = c.sem(ctx, f"{tag}_turned")
        copied = c.sem(ctx, f"{tag}_copied")
        block = ctx.enter_context(c.nc.Block())
        transpose_tiles(c, block, c.Y, c.XT, tp, None, 0, turned, copied)


def router_phase(c, combine, gate_dram):
    nc = c.nc
    with ExitStack() as ctx:
        W = c.sb(ctx, "gate_w", [P, KD, EXPERTS], F32)
        logits = c.sb(ctx, "logits", [P, NT, EXPERTS], F32)
        best = c.sb(ctx, "best", [P, NT, 8], F32)
        best_at = c.sb(ctx, "best_at", [P, NT, 8], U32)
        at = c.sb(ctx, "best_at_f", [P, NT, 8], F32)
        iota = c.sb(ctx, "expert_no", [P, EXPERTS], F32)
        scores = c.sb(ctx, "scores", [P, NT, EXPERTS], F32)
        chosen = c.sb(ctx, "chosen", [P, 2, NT, EXPERTS], F32)
        total = c.sb(ctx, "score_sum", [P, NT], F32)
        ps = c.ps(ctx, "logit_ps", [P, NT, EXPERTS])
        loaded = c.sem(ctx, "gate_loaded")
        done = c.sem(ctx, "logits_done")
        numbered = c.sem(ctx, "numbered")
        link = c.sem(ctx, "router_link")
        shifted = c.sem(ctx, "logits_shifted")
        exped = c.sem(ctx, "scores_exped")
        block = ctx.enter_context(nc.Block())

        @block.sync
        def _(sp):
            sp.dma_start(W[:, :, :], gate_dram).then_inc(loaded, 16)

        @block.gpsimd
        def _(pool):
            pool.iota(iota[:, :], pattern=[[1, EXPERTS]], base=0, channel_multiplier=0,
                      allow_small_or_imprecise_dtypes=True).then_inc(numbered, 1)

        @block.tensor
        def _(pe):
            pe.wait_ge(loaded, 16)
            for t in range(NT):
                for k in range(KD):
                    last = pe.matmul(ps[:, t, :], c.XT[:, k, t * P:(t + 1) * P], W[:, k, :], start=(k == 0),
                                     stop=(k == KD - 1))
            last.then_inc(done, 1)

        @block.scalar
        def _(act):
            act.wait_ge(shifted, 1)
            act.activation(flat(scores[:, :, :]), flat(logits[:, :, :]), ACT.Exp).then_inc(exped, 1)

        @block.vector
        def _(dve):
            n = [0]

            def linked(ins):
                n[0] += 1
                ins.then_inc(link, 1)
                dve.wait_ge(link, n[0])

            def over_experts(ap):
                return ap.unsqueeze(2).broadcast_to([P, NT, EXPERTS])

            dve.memset(combine[:, :, EXPERTS:ALL_EXPERTS], 1.0)
            dve.wait_ge(done, 1)
            linked(dve.tensor_copy(logits[:, :, :], ps[:, :, :]))
            for t in range(NT):
                last = dve.max(best[:, t, :], logits[:, t, :])
            linked(last)
            for t in range(NT):
                last = dve.max_index(best_at[:, t, :], best[:, t, :], logits[:, t, :])
            linked(last)
            dve.tensor_copy(at[:, :, :], best_at[:, :, :])
            dve.tensor_tensor(logits[:, :, :], logits[:, :, :], over_experts(best[:, :, 0]),
                              ALU.subtract).then_inc(shifted, 1)
            dve.wait_ge(numbered, 1)
            dve.wait_ge(exped, 1)
            linked(dve.tensor_reduce(total[:, :], scores[:, :, :], AX.X, ALU.add))
            linked(dve.reciprocal(total[:, :], total[:, :]))
            for i in range(2):
                last = dve.tensor_tensor(chosen[:, i, :, :], iota[:, :].unsqueeze(1).broadcast_to([P, NT, EXPERTS]),
                                         over_experts(at[:, :, i]), ALU.is_equal)
            linked(last)
            linked(dve.tensor_tensor(chosen[:, 0, :, :], chosen[:, 0, :, :], chosen[:, 1, :, :], ALU.add))
            linked(dve.tensor_tensor(scores[:, :, :], scores[:, :, :], over_experts(total[:, :]), ALU.mult))
            dve.tensor_tensor(combine[:, :, 0:EXPERTS], scores[:, :, :], chosen[:, 0, :, :], ALU.mult)


def moe_phase(c, combine, wgu_dram, wdn_dram):
    nc = c.nc
    GROUP = 4
    groups = [range(g, min(g + GROUP, HT)) for g in range(0, HT, GROUP)]
    last_expert = [min(-(-(g[-1] + 1) * P // INTER), ALL_EXPERTS) - 1 for g in groups]
    with ExitStack() as ctx:
        wgu = c.sb(ctx, "w_gate_up", [P, KD, ALL_EXPERTS, 2 * INTER], F32)
        wdn = c.sb(ctx, "w_down", [P, HT, D], F32)
        xs = [c.sb(ctx, f"moe_x{i}", [P, KD, P], F32) for i in range(2)]
        sg = [c.sb(ctx, f"moe_silu{i}", [P, INTER], F32) for i in range(2)]
        hcat = c.sb(ctx, "hidden", [P, HT * P], F32)
        ht = c.sb(ctx, "hidden_t", [P, HT, P], F32)
        gu_ps = [c.ps(ctx, f"gu_ps{i}", [P, 512]) for i in range(3)]
        tp = [c.ps(ctx, f"hidden_tp{i}", [P, GROUP, P]) for i in range(2)]
        y_ps = c.ps(ctx, "moe_y_ps", [P, 512])
        s = {n: c.sem(ctx, n) for n in (
            "wgu_in", "wdn_in", "moe_x_ready", "moe_x_free", "pad_zeroed", "gu_done", "silu_done", "gu_free",
            "hidden_turned", "hidden_copied", "y_done", "y_free")}
        block = ctx.enter_context(nc.Block())

        @block.sync
        def _(sp):
            for e in range(0, ALL_EXPERTS, 3):
                sp.dma_start(wgu[:, :, e:e + 3, :], wgu_dram[:, :, e:e + 3, :]).then_inc(s["wgu_in"], 16)
            sp.dma_start(wdn[:, :, :], wdn_dram).then_inc(s["wdn_in"], 16)

        @block.gpsimd
        def _(pool):
            pool.sem_inc(s["moe_x_free"], 2)
            pool.memset(hcat[:, HCAT:HT * P], 0.0).then_inc(s["pad_zeroed"], 1)
            with pool.Fori(0, NT // 2) as i:
                for j in range(2):
                    t = 2 * i + j
                    pool.wait_ge(s["moe_x_free"], t + 1)
                    pool.tensor_copy(xs[j][:, :, :], c.XT[:, :, ds(t * P, P)]).then_inc(s["moe_x_ready"], 1)

        @block.tensor
        def _(pe):
            pe.sem_inc(s["gu_free"], 3)
            pe.sem_inc(s["hidden_copied"], 2)
            pe.wait_ge(s["wgu_in"], 16 * (ALL_EXPERTS // 3))
            pe.wait_ge(s["wdn_in"], 16)
            pe.wait_ge(s["pad_zeroed"], 1)

            def up(t, x, e):
                pe.wait_ge(s["gu_free"], ALL_EXPERTS * t + e + 1)
                for k in range(KD):
                    last = pe.matmul(gu_ps[e % 3][:, 0:2 * INTER], x[:, k, :], wgu[:, k, e, :], start=(k == 0),
                                     stop=(k == KD - 1))
                last.then_inc(s["gu_done"], 1)

            def turn(t, g):
                pe.wait_ge(s["gu_free"], ALL_EXPERTS * t + last_expert[g] + 1 + 3)
                pe.wait_ge(s["hidden_copied"], len(groups) * t + g + 1)
                for n, k in enumerate(groups[g]):
                    last = pe.transpose(tp[g % 2][:, n, :], hcat[:, k * P:(k + 1) * P], c.ident[:, :])
                last.then_inc(s["hidden_turned"], 1)

            def down(t, g):
                pe.wait_ge(s["hidden_copied"], len(groups) * t + g + 1 + 2)
                if g == 0:
                    pe.wait_ge(s["y_free"], t + 1)
                for k in groups[g]:
                    last = pe.matmul(y_ps[:, 0:D], ht[:, k, :], wdn[:, k, :], start=(k == 0), stop=(k == HT - 1))
                if g == len(groups) - 1:
                    last.then_inc(s["y_done"], 1)

            with pe.Fori(0, NT // 2) as i:
                for j in range(2):
                    t = 2 * i + j
                    pe.wait_ge(s["moe_x_ready"], t + 1)
                    turned = downed = 0
                    for e in range(ALL_EXPERTS + 2):
                        if e < ALL_EXPERTS:
                            up(t, xs[j], e)
                        if downed < turned:
                            down(t, downed)
                            downed += 1
                        if turned < len(groups) and last_expert[turned] <= e - 2:
                            turn(t, turned)
                            turned += 1
                    while downed < len(groups):
                        if turned < len(groups):
                            turn(t, turned)
                            turned += 1
                        down(t, downed)
                        downed += 1

        @block.scalar
        def _(act):
            with act.Fori(0, NT // 2) as i:
                for j in range(2):
                    t = 2 * i + j
                    for e in range(ALL_EXPERTS):
                        n = ALL_EXPERTS * t + e
                        act.wait_ge(s["gu_done"], n + 1)
                        act.wait_ge(s["gu_free"], n + 2)
                        act.activation(sg[e % 2][:, :], gu_ps[e % 3][:, 0:INTER], ACT.Silu
                                       ).then_inc(s["silu_done"], 1)

        @block.vector
        def _(dve):
            dve.sem_inc(s["y_free"], 1)

            def copy_hidden(t, g):
                dve.wait_ge(s["hidden_turned"], len(groups) * t + g + 1)
                n = len(groups[g])
                dve.tensor_copy(ht[:, groups[g][0]:groups[g][-1] + 1, :], tp[g % 2][:, 0:n, :]
                                ).then_inc(s["hidden_copied"], 1)

            with dve.Fori(0, NT // 2) as i:
                for j in range(2):
                    t = 2 * i + j
                    copied = 0
                    for e in range(ALL_EXPERTS):
                        n = ALL_EXPERTS * t + e
                        if e == 0:
                            dve.wait_ge(s["y_free"], t + 1)
                        dve.wait_ge(s["silu_done"], n + 1)
                        dve.scalar_tensor_tensor(
                            hcat[:, e * INTER:(e + 1) * INTER], sg[e % 2][:, :],
                            combine[:, ds(t, 1), e:e + 1].rearrange("p a b -> p (a b)"),
                            gu_ps[e % 3][:, INTER:2 * INTER], ALU.mult, ALU.mult).then_inc(s["gu_free"], 1)
                        if copied < len(groups) and last_expert[copied] <= e - 2:
                            copy_hidden(t, copied)
                            copied += 1
                    for g in range(copied, len(groups)):
                        copy_hidden(t, g)
                    dve.wait_ge(s["y_done"], t + 1)
                    dve.tensor_copy(c.Y[:, ds(t, 1), :].rearrange("p a d -> p (a d)"), y_ps[:, 0:D]
                                    ).then_inc(s["y_free"], 1)
                    dve.sem_inc(s["moe_x_free"], 1)


def ffn_phase(c, wg_dram, wu_dram, wd_dram, gs_dram, us_dram, ds_dram):
    nc = c.nc
    NB, B = 4, T // 4
    ZERO_POINT = 128.0
    with ExitStack() as ctx:
        wq = c.sb(ctx, "ffn_int", [P, 3, 2 * FFN], I32)
        w = c.sb(ctx, "ffn_w", [P, 3, 2 * FFN], F32)
        scale = c.sb(ctx, "ffn_scales", [P, 2, FT], F32)
        out_scale = c.sb(ctx, "ffn_out_scale", [P, D], F32)
        sg = [c.sb(ctx, f"ffn_silu{i}", [P, B], F32) for i in range(2)]
        ht = [c.sb(ctx, f"ffn_hidden{i}", [P, FT, B], F32) for i in range(2)]
        g_ps = [c.ps(ctx, f"g_ps{i}", [P, B]) for i in range(2)]
        u_ps = [c.ps(ctx, f"u_ps{i}", [P, B]) for i in range(2)]
        y_ps = [c.ps(ctx, f"ffn_y_ps{i}", [P, 512]) for i in range(2)]
        s = {n: c.sem(ctx, n) for n in (
            "ffn_in", "dequantised", "g_done", "u_done", "ffn_silu_done", "hidden_done", "ffn_y_done", "ffn_y_free")}
        wg = w[:, 0, :].rearrange("p (k n) -> p k n", k=KD)
        wu = w[:, 1, :].rearrange("p (k n) -> p k n", k=KD)
        wd = w[:, 2, :].rearrange("p (k n) -> p k n", k=FT)
        block = ctx.enter_context(nc.Block())

        @block.sync
        def _(sp):
            for i, src in enumerate((wg_dram, wu_dram, wd_dram)):
                sp.dma_start(wq[:, i, :], src).then_inc(s["ffn_in"], 16)
            sp.dma_start(scale[:, 0, :], gs_dram).then_inc(s["ffn_in"], 16)
            sp.dma_start(scale[:, 1, :], us_dram).then_inc(s["ffn_in"], 16)
            sp.dma_start(out_scale[:, :], ds_dram.broadcast_to([P, D])).then_inc(s["ffn_in"], 16)

        @block.tensor
        def _(pe):
            pe.sem_inc(s["hidden_done"], 2)
            pe.sem_inc(s["ffn_y_free"], 2)
            pe.wait_ge(s["dequantised"], 3)
            with pe.Fori(0, NB // 2) as i:
                for j in range(2):
                    b = 2 * i + j
                    for m in range(FT):
                        pe.wait_ge(s["hidden_done"], FT * b + m + 1)
                        for weights, ps, done in ((wg, g_ps, "g_done"), (wu, u_ps, "u_done")):
                            for k in range(KD):
                                last = pe.matmul(ps[m % 2][:, :], weights[:, k, m * P:(m + 1) * P],
                                                 c.XT[:, k, ds(b * B, B)], start=(k == 0), stop=(k == KD - 1))
                            last.then_inc(s[done], 1)
                    for q in range(B // P):
                        pe.wait_ge(s["hidden_done"], FT * b + FT + 2)
                        pe.wait_ge(s["ffn_y_free"], (B // P) * b + q + 1)
                        for m in range(FT):
                            last = pe.matmul(y_ps[q % 2][:, 0:D], ht[j][:, m, q * P:(q + 1) * P], wd[:, m, :],
                                             start=(m == 0), stop=(m == FT - 1))
                        last.then_inc(s["ffn_y_done"], 1)

        @block.scalar
        def _(act):
            act.wait_ge(s["ffn_in"], 96)
            with act.Fori(0, NB // 2) as i:
                for j in range(2):
                    for m in range(FT):
                        n = FT * (2 * i + j) + m
                        act.wait_ge(s["g_done"], n + 1)
                        act.wait_ge(s["hidden_done"], n + 1)
                        act.activation(sg[m % 2][:, :], g_ps[m % 2][:, :], ACT.Silu, scale=scale[:, 0, m:m + 1]
                                       ).then_inc(s["ffn_silu_done"], 1)

        @block.vector
        def _(dve):
            dve.wait_ge(s["ffn_in"], 96)
            for i in range(3):
                dve.tensor_scalar(w[:, i, :], wq[:, i, :], ZERO_POINT, None, ALU.subtract
                                  ).then_inc(s["dequantised"], 1)
            with dve.Fori(0, NB // 2) as i:
                for j in range(2):
                    b = 2 * i + j
                    for m in range(FT):
                        n = FT * b + m
                        dve.wait_ge(s["ffn_silu_done"], n + 1)
                        dve.wait_ge(s["u_done"], n + 1)
                        dve.scalar_tensor_tensor(ht[j][:, m, :], u_ps[m % 2][:, :], scale[:, 1, m:m + 1],
                                                 sg[m % 2][:, :], ALU.mult, ALU.mult).then_inc(s["hidden_done"], 1)
                    for q in range(B // P):
                        dve.wait_ge(s["ffn_y_done"], (B // P) * b + q + 1)
                        dve.tensor_tensor(c.Y[:, ds((B // P) * b + q, 1), :].rearrange("p a d -> p (a d)"),
                                          y_ps[q % 2][:, 0:D], out_scale[:, :], ALU.mult
                                          ).then_inc(s["ffn_y_free"], 1)


HK, HV, DK = 16, 32, 128
VH = HV // HK
KCONV = 4
QC = 4
QT_ = QC * P
NQ = NT // QC
NM = QC * VH
GM = NM // 2
CH = 2 + VH
BLOCK = 4
EPS = 1e-6
TINY = 1e-18
GRID = 1e-11
W_CONV = KD * (CH + VH) * DK
W_OUT = W_CONV + CH * KCONV
W_ALL = W_OUT + VH * D

UNITS = ["b", "b2", "im", "y2", "r0", "x0", "n0", "r1", "x1", "n1", "r2", "x2", "n2", "r3", "x3", "n3",
         "r4", "x4", "n4"]
NEWTON = 5
BY_DVE = {"im", "b2", "y2"} | {f"{x}{i}" for x in "rn" for i in range(NEWTON)}
NU = len(UNITS)
NU_DVE = len(BY_DVE)
NU_ACT = NU - NU_DVE
FRONT_STEPS = NU
PROJECT_AT = (0, 1, 2, 3, 4, 5)
CONV_AT = [min(max(step - 3, 0), KCONV * CH) for step in range(FRONT_STEPS)] + [KCONV * CH]
PIECES = 4 * (QC + 1)


def copied_by(name):
    i = UNITS.index(name)
    mine = name in BY_DVE
    return mine, sum((u in BY_DVE) == mine for u in UNITS[:i + 1])


def delta_tables(c, tab, a):
    nc = c.nc
    with ExitStack() as ctx:
        W = c.sb(ctx, "w_ab", [P, KD, 2 * HV], F32)
        bias = c.sb(ctx, "gate_bias", [P, 2, HV], F32)
        y = c.sb(ctx, "gate_y", [P, NT, HV], F32)
        tmp = c.sb(ctx, "gate_tmp", [P, NT, HV], F32)
        ab = [c.ps(ctx, f"ab_ps{i}", [P, NT // 2, 2 * HV]) for i in range(2)]
        sums = [c.ps(ctx, f"sum_ps{i}", [P, NT, HV]) for i in range(3)]
        s = {n: c.sem(ctx, n) for n in ("ab_in", "ab_done", "gate_link", "act_link", "summed", "masks_done")}
        block = ctx.enter_context(nc.Block())

        @block.sync
        def _(sp):
            sp.dma_start(W[:, :, :], a["w_ab"]).then_inc(s["ab_in"], 16)
            sp.dma_start(bias[:, 0, :], a["dt_bias"].broadcast_to([P, HV])).then_inc(s["ab_in"], 16)
            sp.dma_start(bias[:, 1, :], a["a_log"].broadcast_to([P, HV])).then_inc(s["ab_in"], 16)
            sp.dma_start(tab["norm_w"], a["norm_w"].broadcast_to([P, DK])).then_inc(s["ab_in"], 16)

        @block.gpsimd
        def _(pool):
            n = [0]

            def linked(ins):
                n[0] += 1
                ins.then_inc(s["masks_done"], 1)
                pool.wait_ge(s["masks_done"], n[0])

            for name in ("upto", "after", "before", "block"):
                linked(pool.memset(tab[name], 1.0))
            linked(pool.memset(tab["neg"], -30000.0))
            linked(pool.memset(tab["ones"], 1.0))
            linked(pool.memset(tab["halo"], 1.0))
            linked(pool.memset(tab["half"], 0.5))
            linked(pool.memset(tab["mhalf"], -0.5))
            linked(pool.memset(tab["halo"][:, 0:1], 0.0))
            sel = lambda ap, pattern, base, mult, op: linked(pool.affine_select(
                out=ap, in_=ap, compare_op=op, fill=0.0, base=base, pattern=pattern, channel_multiplier=mult))
            sel(tab["upto"], [[1, P]], 0, -1, ALU.is_ge)
            sel(tab["after"], [[-1, P]], 0, 1, ALU.is_gt)
            sel(tab["before"], [[1, P]], 0, -1, ALU.is_gt)
            sel(tab["neg"], [[-1, P]], 0, 1, ALU.is_gt)
            blocks = tab["block"].rearrange("p (b c) -> p b c", c=BLOCK)
            sel(tab["block"], [[1, P]], 0, -1, ALU.is_gt)
            sel(blocks, [[-BLOCK, P // BLOCK], [0, BLOCK]], 0, 1, ALU.is_ge)
            sel(blocks, [[BLOCK, P // BLOCK], [0, BLOCK]], BLOCK - 1, -1, ALU.is_ge)

        @block.tensor
        def _(pe):
            pe.wait_ge(s["ab_in"], 64)
            for t in range(NT):
                for k in range(KD):
                    last = pe.matmul(ab[t // 8][:, t % 8, :], c.XT[:, k, t * P:(t + 1) * P], W[:, k, :],
                                     start=(k == 0), stop=(k == KD - 1))
            last.then_inc(s["ab_done"], 1)
            pe.wait_ge(s["masks_done"], 17)
            pe.wait_ge(s["gate_link"], 7)
            for i, m in enumerate(("upto", "after", "ones")):
                last = pe.matmul(flat(sums[i][:, :, :]), tab[m], flat(tab["g"]), start=True, stop=True)
            last.then_inc(s["summed"], 1)

        @block.scalar
        def _(act):
            def linked(ins, n):
                ins.then_inc(s["act_link"], 1)
                act.wait_ge(s["act_link"], n)

            act.wait_ge(s["ab_in"], 64)
            linked(act.activation(bias[:, 1, :], bias[:, 1, :], ACT.Exp), 1)
            act.wait_ge(s["gate_link"], 3)
            linked(act.activation(flat(tmp[:, :, :]), flat(tmp[:, :, :]), ACT.Exp), 2)
            linked(act.activation(flat(tab["nbeta"]), flat(tab["nbeta"]), ACT.Exp), 3)
            linked(act.activation(flat(tmp[:, :, :]), flat(tmp[:, :, :]), ACT.Ln, bias=1.0), 4)
            act.wait_ge(s["summed"], 1)
            for i, name in enumerate(("neg_decay", "decay_after", "chunk_decay")):
                linked(act.activation(flat(tab[name]), flat(sums[i][:, :, :]), ACT.Exp), 5 + i)

        @block.vector
        def _(dve):
            def linked(ins, n):
                ins.then_inc(s["gate_link"], 1)
                dve.wait_ge(s["gate_link"], n)

            heads = lambda ap: ap.unsqueeze(1).broadcast_to([P, NT, HV])
            dve.wait_ge(s["ab_done"], 1)
            for i in range(2):
                half = slice(8 * i, 8 * i + 8)
                dve.tensor_scalar(tab["nbeta"][:, half, :], ab[i][:, :, 0:HV], -1.0, None, ALU.mult)
                last = dve.tensor_tensor(y[:, half, :], ab[i][:, :, HV:2 * HV],
                                         bias[:, 0, :].unsqueeze(1).broadcast_to([P, 8, HV]), ALU.add)
            linked(last, 1)
            linked(dve.tensor_scalar(tmp[:, :, :], y[:, :, :], -1.0, None, ALU.mult), 2)
            linked(dve.tensor_tensor(tmp[:, :, :], tmp[:, :, :], y[:, :, :], ALU.min), 3)
            dve.wait_ge(s["act_link"], 4)
            linked(dve.scalar_tensor_tensor(y[:, :, :], y[:, :, :], 0.0, tmp[:, :, :], ALU.max, ALU.add), 4)
            dve.tensor_scalar(tab["nbeta"], tab["nbeta"], 1.0, None, ALU.add)
            linked(dve.tensor_scalar(y[:, :, :], y[:, :, :], -1.0, None, ALU.mult), 5)
            linked(dve.tensor_tensor(tab["g"], y[:, :, :], heads(bias[:, 1, :]), ALU.mult), 6)
            linked(dve.reciprocal(tab["nbeta"], tab["nbeta"]), 7)
            linked(dve.tensor_scalar(tab["nbeta"], tab["nbeta"], -1.0, None, ALU.mult), 8)
            dve.wait_ge(s["act_link"], 7)
            linked(dve.tensor_scalar(tab["neg_decay"], tab["neg_decay"], -1.0, None, ALU.mult), 9)
            dve.memset(tab["neg_decay"][:, 0, :], 0.0)
            dve.memset(tab["chunk_decay"][:, 0, :], 0.0)
            dve.tensor_scalar(tab["norm_w"], tab["norm_w"], -1.0, None, ALU.mult)


def delta_phase(c, a):
    nc = c.nc
    with ExitStack() as outer:
        f = lambda name, shape, dt=F32: c.sb(outer, "t_" + name, shape, dt)
        tab = {}
        for name in ("g", "nbeta", "neg_decay", "decay_after", "chunk_decay"):
            tab[name] = f(name, [P, NT, HV])[:, :, :]
        for name in ("upto", "after", "before", "block", "ones", "norm_w"):
            tab[name] = f(name, [P, P])[:, :]
        tab["neg"] = f("neg", [P, P], BF16)[:, :]
        tab["halo"] = f("halo", [P, NQ])[:, :]
        tab["half"] = f("half", [P, NM])[:, :]
        tab["mhalf"] = f("mhalf", [P, NM])[:, :]
        delta_tables(c, tab, a)
        delta_heads(c, tab, a)


def delta_heads(c, tab, a):
    nc = c.nc
    with ExitStack() as ctx:
        f = lambda name, shape, dt=F32: c.sb(ctx, "dl_" + name, shape, dt)
        landing = f("landing", [P, W_ALL])
        ws = f("weights", [P, W_ALL])
        wqkvz = ws[:, 0:W_CONV].rearrange("p (k m n) -> p k m n", k=KD, n=DK)
        conv_w = ws[:, W_CONV:W_OUT].rearrange("p (m k) -> p m k", k=KCONV)
        w_out = ws[:, W_OUT:W_ALL].rearrange("p (a n) -> p a n", a=VH)
        xs = f("x", [P, KD, QT_])
        raw = f("raw", [P, CH, KCONV - 1 + QT_])
        cv = f("conv", [P, CH, QT_])
        kq_ = [f(f"kq{i}", [P, 2, QT_]) for i in range(2)]
        zs = f("z", [P, QC, VH, DK])
        zn_ = [f(f"z_normed{i}", [P, QC, VH, DK]) for i in range(2)]
        kt_ = [f(f"k_tok{i}", [P, QC, DK]) for i in range(2)]
        junk = f("junk", [P, 12, DK])
        sumsq = f("sumsq", [P, 2, QC])
        nsq = f("nsq", [P, QC])
        norm_k = f("norm_k", [P, QC])
        rn = f("inv_nsq", [P, QC])
        sn_ = [f(f"s{i}", [P, QC, VH]) for i in range(2)]
        snd_ = [f(f"s_decayed{i}", [P, QC, VH]) for i in range(2)]
        nd_ = [f(f"neg_decay_q{i}", [P, QC, VH]) for i in range(2)]
        cd_ = [f(f"chunk_decay_q{i}", [P, QC, VH]) for i in range(2)]
        qe_ = [f(f"q_eps{i}", [P, QC]) for i in range(2)]
        vr_ = [f(f"v_scaled{i}", [P, QC, VH, DK]) for i in range(2)]
        gu = f("g_upto", [P, NM, P])
        attn_ = [[f(f"attn{i}{g}", [P, GM, P]) for g in range(2)] for i in range(2)]
        final = [[f(f"inverse{i}{g}", [P, GM, P]) for g in range(2)] for i in range(2)]
        out_cur = f("w_out_cur", [P, VH, D])
        lm = [f(f"l{g}", [P, GM, P]) for g in range(2)]
        buf = [{n: f(f"{n}_{g}", [P, GM, P]) for n in ("a", "b", "im", "x", "b2", "yb")} for g in range(2)]
        eye2 = f("two_ident", [P, P])
        S = f("state", [P, VH, DK])
        r0 = f("r", [P, VH, DK])
        v2 = f("v2", [P, VH, DK])
        v3 = f("v3", [P, VH, DK])
        tq = [f(f"q_state{i}", [P, VH, DK]) for i in range(2)]
        on = [f(f"core{i}", [P, VH, DK]) for i in range(2)]
        ms = [f(f"meansq{i}", [P, VH]) for i in range(2)]
        osc = [f(f"out_scale{i}", [P, VH]) for i in range(2)]
        gated = [f(f"gated{i}", [P, VH, DK]) for i in range(2)]
        gt = [f(f"gated_t{i}", [P, VH, P]) for i in range(2)]
        prep = [c.ps(ctx, f"prep{i}", [P, 4, P]) for i in range(2)]
        inv = [[c.ps(ctx, f"inv{g}{i}", [P, GM, P]) for i in range(2)] for g in range(2)]
        ra = c.ps(ctx, "rec_a", [P, 2, VH, DK])
        rb = c.ps(ctx, "rec_b", [P, 2, VH, DK])
        names = ("halo_done", "flushed", "y2_sum", "w_landed", "w_ready", "w_taken", "x_ready", "raw_done", "raw_free", "conv_step", "silu_done",
                 "prep_mm", "prep_act", "prep_dve", "zn_done", "sq_k", "scal", "nsq_done", "norm_done", "gu_done",
                 "lraw_done", "masked", "y1_done", "inv_mm0", "inv_mm1", "inv_act0", "inv_act1", "inv_dve0",
                 "inv_dve1", "ks_done", "r_done", "tq_done", "u_done", "v3_done", "v2_done", "sv_done", "av_done",
                 "s_done", "o_done", "o_sq", "osc_link", "osc_done", "gated_done", "gt_done", "gt_copied",
                 "y_done", "y_added", "quad_done", "zeroed", "out_cur_done", "rotated", "diag_done")
        s = {n: c.sem(ctx, "dn_" + n) for n in names}
        block = ctx.enter_context(nc.Block())

        def group(p, g):
            return {**buf[g], "ya": final[p][g], "f": buf[g]["b"]}

        OPERANDS = {"b2": ("a", "b"), "y2": ("b2", "ya")}
        TURNS = {"b": "a"}
        OUT = {"b": "b", "im": "im", "b2": "b2", "y2": "yb"}
        NEEDS = {"b2": ["b"], "y2": ["b2"]}
        for i in range(NEWTON):
            old, new = ("yb", "ya") if i % 2 == 0 else ("ya", "yb")
            before = "y2" if i == 0 else f"n{i - 1}"
            OPERANDS[f"r{i}"], OPERANDS[f"n{i}"], TURNS[f"x{i}"] = ("im", old), ("x", "f"), old
            OUT.update({f"r{i}": "f", f"x{i}": "x", f"n{i}": new})
            NEEDS.update({f"r{i}": ["im", before], f"x{i}": [before], f"n{i}": [f"r{i}", f"x{i}"]})

        def copied(engine, g, names, n):
            by = [copied_by(name) for name in names]
            dve = max([k for mine, k in by if mine], default=0)
            act = max([k for mine, k in by if not mine], default=0)
            if dve:
                engine.wait_ge(s[f"inv_dve{g}"], NU_DVE * n + 1 + dve)
            if act:
                engine.wait_ge(s[f"inv_act{g}"], NU_ACT * n + act)

        def over_quads(engine, front, back, head=None, flush=None):
            with engine.Fori(0, HK) as kh:
                if head:
                    head(kh)
                for step in range(-1, FRONT_STEPS):
                    front(step, kh, 0, NQ * kh, 0)
                for q in range(NQ):
                    n = NQ * kh + q
                    ahead = None
                    if q < NQ - 1:
                        ahead = lambda step: front(step, kh, q + 1, n + 1, (q + 1) % 2)
                    back(kh, q, n, q % 2, ahead)
            for i in range(PIECES):
                flush(i)

        def both(ap):
            return ap.unsqueeze(2).broadcast_to([P, VH, DK])

        @block.sync
        def _(sp):
            sp.sem_inc(s["w_taken"], 1)
            with sp.Fori(0, HK) as kh:
                sp.wait_ge(s["w_taken"], kh + 1)
                sp.dma_start(landing[:, :], a["w_delta"][ds(kh, 1), :, :].rearrange("a p n -> (a p) n")
                             ).then_inc(s["w_landed"], 16)

        @block.tensor
        def _(pe):
            pe.sem_inc(s["prep_act"], 10)
            pe.sem_inc(s["prep_dve"], 4)
            pe.sem_inc(s["s_done"], 1)
            pe.sem_inc(s["gt_copied"], 4)
            pe.sem_inc(s["y_added"], 4)
            pe.sem_inc(s["inv_dve0"], 1)
            pe.sem_inc(s["out_cur_done"], 1)
            pe.sem_inc(s["inv_dve1"], 1)
            pe.wait_ge(s["zeroed"], 1)

            def prep_unit(n, u, mms):
                if u in (0, 1):
                    pe.wait_ge(s["prep_dve"], 4 * n + 3 + u)
                elif u in (12, 13):
                    pe.wait_ge(s["prep_dve"], 4 * n + 4 + u - 11)
                else:
                    pe.wait_ge(s["prep_act"], 10 * n + 10 + u - 1)
                mms(prep[u % 2]).then_inc(s["prep_mm"], 1)

            def front(step, kh, q, n, p):
                if step == 0:
                    pe.wait_ge(s["w_ready"], kh + 1)
                    pe.wait_ge(s["x_ready"], n + 1)
                    if q == 0:
                        outputs_left(n)
                if step in PROJECT_AT[:CH]:
                    m = PROJECT_AT.index(step)

                    def project(bank):
                        for k in range(KD):
                            last = pe.matmul(flat(bank[:, :, :]), wqkvz[:, k, m, :], xs[:, k, :], start=(k == 0),
                                             stop=(k == KD - 1))
                        return last
                    prep_unit(n, m, project)
                if step in PROJECT_AT[CH:]:
                    i = PROJECT_AT.index(step) - CH

                    def project_z(bank):
                        for j in range(2):
                            for k in range(KD):
                                last = pe.matmul(flat(bank[:, 2 * j:2 * j + 2, :]),
                                                 xs[:, k, (2 * i + j) * P:(2 * i + j + 1) * P],
                                                 flat(wqkvz[:, k, CH:CH + VH, :]), start=(k == 0),
                                                 stop=(k == KD - 1))
                        return last
                    prep_unit(n, 4 + i, project_z)

            def outputs_left(n):
                pe.wait_ge(s["gt_copied"], 4 * n + 4)
                pe.wait_ge(s["y_added"], 4 * n + 4)

            def back(kh, q, n, p, ahead):
                kq = kq_[p]
                if q:
                    outputs_left(n)
                for g in range(2):
                    pe.wait_ge(s["gu_done"], n + 1)

                    def decays(bank, g=g):
                        pe.matmul(flat(bank[:, :, :]), tab["after"], flat(gu[:, GM * g:GM * g + GM, :]),
                                  start=True, stop=False)
                        return pe.matmul(bank[:, :, :], c.identb[:, :],
                                         tab["neg"].unsqueeze(1).broadcast_to([P, GM, P]), start=False, stop=True)
                    prep_unit(n, 6 + g, decays)
                for i in range(2):
                    pe.wait_ge(s["silu_done"], 4 * n + 4)

                    def turn_kq(bank, i=i):
                        for j in range(2):
                            for x in range(2):
                                last = pe.transpose(bank[:, 2 * j + x, :], kq[:, x, (2 * i + j) * P:(2 * i + j + 1) * P],
                                                    c.ident[:, :])
                        return last
                    prep_unit(n, 8 + i, turn_kq)
                for i in range(2):
                    pe.wait_ge(s["silu_done"], 4 * n + 2)

                    def turn_v(bank, i=i):
                        for j in range(2):
                            for h in range(VH):
                                last = pe.transpose(bank[:, 2 * j + h, :], cv[:, 2 + h, (2 * i + j) * P:(2 * i + j + 1) * P],
                                                    c.ident[:, :])
                        return last
                    prep_unit(n, 10 + i, turn_v)
                for i in range(2):
                    def products(bank, i=i):
                        for j in range(2):
                            cols = slice((2 * i + j) * P, (2 * i + j + 1) * P)
                            last = pe.matmul(bank[:, 2 * j:2 * j + 2, :], kq[:, 0, cols], kq[:, :, cols],
                                             start=True, stop=True)
                        return last
                    prep_unit(n, 12 + i, products)

                def unit(g, u):
                    name, B = UNITS[u], group(p, g)
                    copied(pe, g, NEEDS.get(name, []) + UNITS[max(u - 2, 0):max(u - 1, 0)], n)
                    if name == "b":
                        pe.wait_ge(s["diag_done"], 2 * n + g + 1)
                    if name == "im":
                        pe.wait_ge(s["masked"], 2 * n + g + 1)
                    if name == "y2":
                        pe.wait_ge(s["y1_done"], 2 * n + g + 1)
                    bank = inv[g][u % 2]
                    for m in range(GM):
                        if name == "im":
                            last = pe.transpose(bank[:, m, :], lm[g][:, m, :], c.ident[:, :])
                        elif name in TURNS:
                            last = pe.transpose(bank[:, m, :], B[TURNS[name]][:, m, :], c.ident[:, :])
                        else:
                            w, x = OPERANDS[name]
                            last = pe.matmul(bank[:, m, :], B[w][:, m, :], B[x][:, m, :], start=True, stop=True)
                    last.then_inc(s[f"inv_mm{g}"], 1)

                for g in range(2):
                    pe.wait_ge(s[f"inv_dve{g}"], NU_DVE * n + 1)
                for u in range(NU):
                    for g in range(2):
                        unit(g, u)
                    if ahead:
                        ahead(u)
                    piece(u, n, p, more=bool(ahead))
                for i in range(NU, PIECES):
                    piece(i, n, p)

            def piece(i, n, p, busy=True, more=False):
                ch, stage = divmod(i, 4)
                m = QC * n + ch
                kq, kt, attn, inverse = kq_[1 - p], kt_[1 - p], attn_[1 - p], final[1 - p]
                cols = slice(ch * P, (ch + 1) * P)
                g, j = ch // 2, VH * (ch % 2)
                if stage == 0 and ch < QC:
                    pe.wait_ge(s["s_done"], m + 1)
                    pe.matmul(flat(ra[:, 0, :, :]), kq[:, 0, cols], flat(S[:, :, :]), start=True, stop=True)
                    pe.matmul(flat(ra[:, 1, :, :]), kq[:, 1, cols], flat(S[:, :, :]), start=True, stop=True
                              ).then_inc(s["ks_done"], 1)
                if stage == 1 and ch < QC:
                    pe.wait_ge(s["r_done"], m + 1)
                    for h in range(VH):
                        last = pe.matmul(rb[:, 0, h, :], inverse[g][:, j + h, :], r0[:, h, :], start=True, stop=True)
                    last.then_inc(s["u_done"], 1)
                if stage == 1 and ch:
                    pe.wait_ge(s["gated_done"], m)
                    pe.wait_ge(s["gt_copied"], m + 3)
                    if busy and ch == 1:
                        pe.wait_ge(s["prep_dve"], 4 * n + 8)
                        if more:
                            pe.wait_ge(s["prep_act"], 10 * (n + 1) + 16)
                    for h in range(VH):
                        last = pe.transpose(prep[0][:, h, :], gated[(ch - 1) % 2][:, h, :], c.ident[:, :])
                    last.then_inc(s["gt_done"], 1)
                if stage == 2 and ch < QC:
                    pe.wait_ge(s["v3_done"], m + 1)
                    pe.wait_ge(s["tq_done"], m + 1)
                    pe.matmul(flat(ra[:, 0, :, :]), kt[:, ch, :], flat(v3[:, :, :]), start=True, stop=True
                              ).then_inc(s["sv_done"], 1)
                    pe.wait_ge(s["v2_done"], m + 1)
                    for h in range(VH):
                        last = pe.matmul(rb[:, 1, h, :], attn[g][:, j + h, :], v2[:, h, :], start=True, stop=True)
                    last.then_inc(s["av_done"], 1)
                if stage == 2 and ch:
                    pe.wait_ge(s["gt_copied"], m + 4)
                    pe.wait_ge(s["y_added"], m + 3)
                    pe.wait_ge(s["out_cur_done"], n + 1)
                    for h in range(VH):
                        last = pe.matmul(flat(prep[1][:, 0:2, :]), gt[(ch - 1) % 2][:, h, :], out_cur[:, h, :],
                                         start=(h == 0), stop=(h == VH - 1))
                    last.then_inc(s["y_done"], 1)

            def flush(i):
                if i == 0:
                    for g in range(2):
                        pe.wait_ge(s[f"inv_dve{g}"], NU_DVE * HK * NQ + 1)
                piece(i, HK * NQ, 0, busy=False)

            over_quads(pe, front, back, flush=flush)

        @block.scalar
        def _(act):
            act.sem_inc(s["quad_done"], 1)
            act.wait_ge(s["zeroed"], 1)

            def front(step, kh, q, n, p):
                if step == -1:
                    if q:
                        act.wait_ge(s["prep_mm"], 14 * n - 8)
                    else:
                        act.wait_ge(s["quad_done"], n + 1)
                    act.activation(xs[:, :, :], c.XT[:, :, QT_ * q:QT_ * (q + 1)], ACT.Copy).then_inc(s["x_ready"], 1)
                if step == 0:
                    act.wait_ge(s["raw_free"], n + 1)
                    act.activation(raw[:, :, 0:KCONV - 1], raw[:, :, QT_:QT_ + KCONV - 1], ACT.Copy,
                                   scale=tab["halo"][:, ds(q, 1)]).then_inc(s["halo_done"], 1)
                    act.wait_ge(s["halo_done"], n + 1)
                if step in PROJECT_AT[:CH]:
                    m = PROJECT_AT.index(step)
                    act.wait_ge(s["prep_mm"], 14 * n + m + 1)
                    act.activation(raw[:, m, KCONV - 1:], flat(prep[m % 2][:, :, :]), ACT.Copy
                                   ).then_inc(s["prep_act"], 1)
                if step in PROJECT_AT[CH:]:
                    i = PROJECT_AT.index(step) - CH
                    if i == 0:
                        act.wait_ge(s["zn_done"], n + 1)
                    act.wait_ge(s["prep_mm"], 14 * n + 5 + i)
                    act.activation(flat(zs[:, 2 * i:2 * i + 2, :, :]), flat(prep[i][:, :, :]), ACT.Silu
                                   ).then_inc(s["prep_act"], 1)
                if step == FRONT_STEPS - 1:
                    for m in (2, 3):
                        act.wait_ge(s["conv_step"], 16 * n + 13 + m)
                        act.activation(cv[:, m, :], cv[:, m, :], ACT.Silu).then_inc(s["silu_done"], 1)

            def back(kh, q, n, p, ahead):
                kq, kt = kq_[p], kt_[p]
                act.wait_ge(s["quad_done"], n + 1)
                for x in range(2):
                    act.wait_ge(s["conv_step"], 16 * n + 16)
                    act.activation(kq[:, 1 - x, :], cv[:, x, :], ACT.Silu).then_inc(s["silu_done"], 1)
                for g in range(2):
                    act.wait_ge(s["prep_mm"], 14 * n + 7 + g)
                    act.activation(flat(attn_[p][g][:, :, :]), flat(prep[g][:, :, :]), ACT.Exp).then_inc(s["prep_act"], 1)
                for i in range(2):
                    act.wait_ge(s["prep_mm"], 14 * n + 9 + i)
                    bank = prep[i][:, :, :].rearrange("p (j x) d -> p j x d", x=2)
                    for j in range(2):
                        for x in range(2):
                            last = act.activation(junk[:, 4 * i + 2 * j + x, :], bank[:, j, x, :], ACT.Square,
                                                  accum_out=sumsq[:, x, 2 * i + j:2 * i + j + 1])
                    last.then_inc(s["sq_k"], 1)
                    act.activation(kt[:, 2 * i:2 * i + 2, :], bank[:, :, 0, :], ACT.Copy).then_inc(s["prep_act"], 1)

                def unit(g, u):
                    name = UNITS[u]
                    if name in BY_DVE:
                        return
                    act.wait_ge(s[f"inv_mm{g}"], NU * n + u + 1)
                    act.activation(flat(group(p, g)[OUT[name]][:, :, :]), flat(inv[g][u % 2][:, :, :]), ACT.Copy
                                   ).then_inc(s[f"inv_act{g}"], 1)

                if ahead:
                    ahead(-1)
                for u in range(NU):
                    for g in range(2):
                        unit(g, u)
                    if ahead:
                        ahead(u)
                    piece(u, n, p)
                for i in range(NU, PIECES):
                    piece(i, n, p)
                act.wait_ge(s["y_done"], QC * n + QC)
                act.activation(out_cur[:, :, :], w_out, ACT.Copy).then_inc(s["out_cur_done"], 1)

            def piece(i, n, p):
                ch, stage = divmod(i, 4)
                m = QC * n + ch
                nd, qe = nd_[1 - p], qe_[1 - p]
                if stage == 0 and ch < QC:
                    act.wait_ge(s["r_done"], m + 1)
                    for h in range(VH):
                        last = act.activation(tq[ch % 2][:, h, :], ra[:, 1, h, :], ACT.Copy,
                                              scale=nd[:, ch, h:h + 1])
                    last.then_inc(s["tq_done"], 1)
                if stage == 1 and ch:
                    act.wait_ge(s["gt_done"], m)
                    act.activation(flat(gt[(ch - 1) % 2][:, :, :]), flat(prep[0][:, 0:VH, :]), ACT.Copy
                                   ).then_inc(s["gt_copied"], 1)
                if stage == 3 and ch < QC:
                    act.wait_ge(s["o_done"], m + 1)
                    for h in range(VH):
                        last = act.activation(junk[:, 8 + 2 * (ch % 2) + h, :], on[ch % 2][:, h, :], ACT.Square,
                                              accum_out=ms[ch % 2][:, h:h + 1])
                    last.then_inc(s["o_sq"], 1)
                    act.wait_ge(s["o_sq"], m + 1)
                    act.activation(osc[ch % 2][:, :], ms[ch % 2][:, :], ACT.Identity, scale=1.0 / DK,
                                   bias=qe[:, ch:ch + 1]).then_inc(s["osc_link"], 1)

            over_quads(act, front, back, flush=lambda i: piece(i, HK * NQ, 0))

        @block.gpsimd
        def _(pool):
            pool.sem_inc(s["zn_done"], 1)

            def root(n, ch):
                m = QC * n + ch
                pool.wait_ge(s["osc_link"], m + 1)
                pool.tensor_tensor(osc[ch % 2][:, :], osc[ch % 2][:, :], tab["mhalf"][:, 0:VH], ALU.pow
                                   ).then_inc(s["osc_done"], 1)

            def front(step, kh, q, n, p):
                if step == 0:
                    if q:
                        pool.wait_ge(s["prep_mm"], 14 * n - 6)
                    else:
                        pool.wait_ge(s["quad_done"], n + 1)
                    gsl = tab["g"][:, ds(QC * q, QC), ds(VH * kh, VH)].unsqueeze(3).broadcast_to([P, QC, VH, P])
                    mask = tab["upto"].unsqueeze(1).unsqueeze(1).broadcast_to([P, QC, VH, P])
                    pool.tensor_tensor(gu[:, :, :].rearrange("p (c h) i -> p c h i", c=QC), gsl, mask, ALU.mult
                                       ).then_inc(s["gu_done"], 1)

            def back(kh, q, n, p, ahead):
                zn = zn_[p]
                pool.wait_ge(s["quad_done"], n + 1)
                pool.wait_ge(s["nsq_done"], n + 1)
                pool.tensor_tensor(norm_k[:, :], nsq[:, :], tab["half"][:, 0:QC], ALU.pow).then_inc(s["norm_done"], 1)
                pool.wait_ge(s["prep_act"], 10 * n + 10 + 6)
                pool.tensor_tensor(zn[:, :, :, :].rearrange("p c h d -> p (c h) d"),
                                   zs[:, :, :, :].rearrange("p c h d -> p (c h) d"),
                                   tab["norm_w"].unsqueeze(1).broadcast_to([P, NM, DK]), ALU.mult
                                   ).then_inc(s["zn_done"], 1)
                if ahead:
                    ahead(0)
                for g in range(2):
                    pool.wait_ge(s["diag_done"], 2 * n + g + 1)
                    pool.tensor_tensor(lm[g][:, :, :], lm[g][:, :, :],
                                       tab["before"].unsqueeze(1).broadcast_to([P, GM, P]), ALU.mult
                                       ).then_inc(s["masked"], 1)
                    pool.tensor_tensor(final[p][g][:, :, :], buf[g]["a"][:, :, :],
                                       c.ident[:, :].unsqueeze(1).broadcast_to([P, GM, P]), ALU.add
                                       ).then_inc(s["y1_done"], 1)
                for ch in range(QC):
                    root(n, ch)

            def flush(i):
                if i % 4 == 0 and i // 4 < QC:
                    root(HK * NQ, i // 4)

            over_quads(pool, front, back, flush=flush)

        @block.vector
        def _(dve):
            for zero in (S, kq_[1], kt_[1], vr_[1], nd_[1], cd_[1], sn_[1], snd_[1], zn_[1], attn_[1][0], attn_[1][1],
                         final[1][0], final[1][1]):
                dve.memset(zero[(slice(None),) * len(zero.shape)], 0.0)
            dve.memset(qe_[1][:, :], 1.0)
            dve.memset(out_cur[:, :, :], 0.0)
            dve.tensor_scalar(eye2[:, :], c.ident[:, :], 2.0, GRID, ALU.mult, ALU.subtract)
            dve.memset(raw[:, :, :], 0.0)
            dve.memset(c.Y[:, :, :], 0.0).then_inc(s["zeroed"], 1)
            dve.sem_inc(s["raw_free"], 1)
            dve.wait_ge(s["zeroed"], 1)

            def head(kh):
                dve.wait_ge(s["quad_done"], NQ * kh + 1)
                dve.wait_ge(s["out_cur_done"], NQ * kh + 1)
                dve.wait_ge(s["w_landed"], 16 * (kh + 1))
                dve.tensor_copy(ws[:, :], landing[:, :]).then_inc(s["w_ready"], 1)
                dve.wait_ge(s["w_ready"], kh + 1)
                dve.sem_inc(s["w_taken"], 1)

            def front(step, kh, q, n, p):
                for i in range(CONV_AT[max(step, 0)], CONV_AT[step + 1]):
                    k, m = divmod(i, CH)
                    if k == 0:
                        dve.wait_ge(s["prep_act"], 10 * n + 10 + m + 1)
                        ins = dve.tensor_scalar(cv[:, m, :], raw[:, m, 0:QT_], conv_w[:, m, 0:1], None, ALU.mult)
                    else:
                        dve.wait_ge(s["conv_step"], 16 * n + 4 * (k - 1) + m + 1)
                        ins = dve.scalar_tensor_tensor(cv[:, m, :], raw[:, m, k:k + QT_], conv_w[:, m, k:k + 1],
                                                       cv[:, m, :], ALU.mult, ALU.add)
                    ins.then_inc(s["conv_step"], 1)
                if step == FRONT_STEPS - 1:
                    dve.wait_ge(s["conv_step"], 16 * n + 16)
                    dve.sem_inc(s["raw_free"], 1)

            def back(kh, q, n, p, ahead):
                sn, snd, nd, cd, qe, vr, attn = sn_[p], snd_[p], nd_[p], cd_[p], qe_[p], vr_[p], attn_[p]
                for g in range(2):
                    dve.wait_ge(s["prep_act"], 10 * n + 10 + 7 + g)
                    dve.tensor_scalar(flat(attn[g][:, :, :]), flat(attn[g][:, :, :]), TINY, TINY, ALU.max,
                                      ALU.subtract).then_inc(s["flushed"], 1)
                    dve.wait_ge(s["flushed"], 2 * n + g + 1)
                dve.wait_ge(s["sq_k"], 2 * n + 2)
                heads = ds(VH * kh, VH)
                tiles = ds(QC * q, QC)
                dve.tensor_scalar(nsq[:, :], sumsq[:, 0, :], EPS, None, ALU.add).then_inc(s["nsq_done"], 1)
                dve.tensor_scalar(qe[:, :], sumsq[:, 1, :], EPS, EPS * DK, ALU.add, ALU.mult)
                dve.tensor_copy(nd[:, :, :], tab["neg_decay"][:, tiles, heads])
                dve.tensor_copy(cd[:, :, :], tab["chunk_decay"][:, tiles, heads])
                dve.wait_ge(s["nsq_done"], n + 1)
                dve.reciprocal(rn[:, :], nsq[:, :]).then_inc(s["scal"], 1)
                dve.wait_ge(s["scal"], 3 * n + 1)
                dve.tensor_tensor(sn[:, :, :], tab["nbeta"][:, tiles, heads],
                                  rn[:, :].unsqueeze(2).broadcast_to([P, QC, VH]), ALU.mult).then_inc(s["scal"], 1)
                dve.wait_ge(s["scal"], 3 * n + 2)
                dve.tensor_tensor(snd[:, :, :], sn[:, :, :], tab["decay_after"][:, tiles, heads], ALU.mult
                                  ).then_inc(s["scal"], 1)
                dve.wait_ge(s["norm_done"], n + 1)
                for i in range(2):
                    dve.wait_ge(s["prep_mm"], 14 * n + 11 + i)
                    dve.tensor_tensor(vr[:, 2 * i:2 * i + 2, :, :],
                                      prep[i][:, :, :].rearrange("p (c h) d -> p c h d", c=2),
                                      norm_k[:, 2 * i:2 * i + 2].unsqueeze(2).unsqueeze(3).broadcast_to([P, 2, VH, DK]),
                                      ALU.mult).then_inc(s["prep_dve"], 1)
                for g in range(2):
                    dve.wait_ge(s["prep_mm"], 14 * n + 13 + g)
                    bank = prep[g][:, :, :].rearrange("p (j x) d -> p j x d", x=2)
                    for j in range(2):
                        for h in range(VH):
                            last = dve.scalar_tensor_tensor(lm[g][:, VH * j + h, :], attn[g][:, VH * j + h, :],
                                                            sn[:, 2 * g + j, h:h + 1], bank[:, j, 0, :],
                                                            ALU.mult, ALU.mult)
                    last.then_inc(s["lraw_done"], 1)
                    dve.wait_ge(s["lraw_done"], 2 * n + g + 1)
                    dve.tensor_tensor(buf[g]["a"][:, :, :], lm[g][:, :, :],
                                      tab["block"].unsqueeze(1).broadcast_to([P, GM, P]), ALU.mult
                                      ).then_inc(s["diag_done"], 1)
                for g in range(2):
                    bank = prep[g][:, :, :].rearrange("p (j x) d -> p j x d", x=2)
                    dve.tensor_tensor(attn[g][:, :, :].rearrange("p (j h) d -> p j h d", j=2),
                                      attn[g][:, :, :].rearrange("p (j h) d -> p j h d", j=2),
                                      bank[:, :, 1, :].unsqueeze(2).broadcast_to([P, 2, VH, P]), ALU.mult
                                      ).then_inc(s["prep_dve"], 1)

                def unit(g, u):
                    name, B = UNITS[u], group(p, g)
                    if name not in BY_DVE:
                        return
                    dve.wait_ge(s[f"inv_mm{g}"], NU * n + u + 1)
                    out, bank = B[OUT[name]][:, :, :], inv[g][u % 2][:, :, :]
                    eye = c.ident[:, :].unsqueeze(1).broadcast_to([P, GM, P])
                    if name == "im":
                        ins = dve.tensor_tensor(out, bank, eye, ALU.subtract)
                    elif name == "y2":
                        dve.wait_ge(s["y1_done"], 2 * n + g + 1)
                        dve.tensor_tensor(out, B["ya"][:, :, :], bank, ALU.add).then_inc(s["y2_sum"], 1)
                        dve.wait_ge(s["y2_sum"], 2 * n + g + 1)
                        ins = dve.tensor_scalar(out, out, GRID, GRID, ALU.add, ALU.subtract)
                    elif name[0] == "r":
                        ins = dve.scalar_tensor_tensor(out, bank, GRID,
                                                       eye2[:, :].unsqueeze(1).broadcast_to([P, GM, P]),
                                                       ALU.add, ALU.add)
                    else:
                        ins = dve.tensor_scalar(out, bank, GRID, GRID, ALU.add, ALU.subtract)
                    ins.then_inc(s[f"inv_dve{g}"], 1)

                for u in range(NU):
                    for g in range(2):
                        unit(g, u)
                    if ahead:
                        ahead(u)
                    piece(u, q, n, p)
                for i in range(NU, PIECES):
                    piece(i, q, n, p)
                dve.sem_inc(s["quad_done"], 1)

            def piece(i, q, n, p):
                ch, stage = divmod(i, 4)
                m = QC * n + ch
                sn, snd, nd, cd, vr, zn = sn_[1 - p], snd_[1 - p], nd_[1 - p], cd_[1 - p], vr_[1 - p], zn_[1 - p]
                if stage == 0 and ch < QC:
                    dve.wait_ge(s["ks_done"], m + 1)
                    for h in range(VH):
                        last = dve.scalar_tensor_tensor(r0[:, h, :], ra[:, 0, h, :], nd[:, ch, h:h + 1],
                                                        vr[:, ch, h, :], ALU.mult, ALU.add)
                    last.then_inc(s["r_done"], 1)
                if stage == 0 and ch:
                    dve.wait_ge(s["osc_done"], m)
                    dve.wait_ge(s["zn_done"], n + 1)
                    for h in range(VH):
                        last = dve.scalar_tensor_tensor(gated[(ch - 1) % 2][:, h, :], on[(ch - 1) % 2][:, h, :],
                                                        osc[(ch - 1) % 2][:, h:h + 1], zn[:, ch - 1, h, :],
                                                        ALU.mult, ALU.mult)
                    last.then_inc(s["gated_done"], 1)
                if stage == 1 and ch < QC:
                    dve.wait_ge(s["u_done"], m + 1)
                    dve.tensor_tensor(v3[:, :, :], rb[:, 0, :, :], both(snd[:, ch, :]), ALU.mult
                                      ).then_inc(s["v3_done"], 1)
                    dve.tensor_tensor(v2[:, :, :], rb[:, 0, :, :], both(sn[:, ch, :]), ALU.mult
                                      ).then_inc(s["v2_done"], 1)
                if stage == 2 and ch < QC:
                    dve.wait_ge(s["sv_done"], m + 1)
                    for h in range(VH):
                        last = dve.scalar_tensor_tensor(S[:, h, :], S[:, h, :], cd[:, ch, h:h + 1], ra[:, 0, h, :],
                                                        ALU.mult, ALU.subtract)
                    last.then_inc(s["s_done"], 1)
                    dve.wait_ge(s["av_done"], m + 1)
                    dve.tensor_tensor(on[ch % 2][:, :, :], tq[ch % 2][:, :, :], rb[:, 1, :, :], ALU.add
                                      ).then_inc(s["o_done"], 1)
                if stage == 3 and ch:
                    dve.wait_ge(s["y_done"], m)
                    y = c.Y[:, ds(QC * q + ch - 1, 1), :].rearrange("p a d -> p (a d)")
                    dve.tensor_tensor(y, y, flat(prep[1][:, 0:2, :]), ALU.add).then_inc(s["y_added"], 1)

            over_quads(dve, front, back, head, flush=lambda i: piece(i, 0, HK * NQ, 0))
            dve.wait_ge(s["y_added"], 4 + QC * (HK * NQ + 1))
            dve.tensor_copy(flat(gu[:, :, :]).rearrange("p (t d) -> p t d", d=D), c.Y[:, 0:QC, :]).then_inc(s["rotated"], 1)
            for q in range(NQ):
                src = c.Y[:, QC * (q + 1):QC * (q + 2), :] if q < NQ - 1 else flat(gu[:, :, :]).rearrange("p (t d) -> p t d", d=D)
                dve.wait_ge(s["rotated"], q + 1)
                dve.tensor_copy(c.Y[:, QC * q:QC * (q + 1), :], src).then_inc(s["rotated"], 1)


def program(nc, a, out, only=None, upto=None):
    with ExitStack() as ctx:
        c = Core(nc, ctx)
        setup(c, a["x"])
        if only in (None, "attn"):
            norm_phase(c, "ln0", add_branch=False)
            with ExitStack() as attn:
                QT = c.sb(attn, "q_t", [P, HEADS, T], BF16)
                KT = c.sb(attn, "k_t", [P, HEADS, T], BF16)
                V = c.sb(attn, "v", [P, NT, HEADS, DH], F32)
                qkv_phase(c, QT, KT, V, a["wqkv"], a["bqkv"], a["rope"])
                attention_phase(c, QT, KT, V)
            turn_phase(c, "ao")
            projection_phase(c, a["out_w"], a["out_b"])
            if upto == "attn":
                norm_phase(c, "ln1", True, want_t=False, out_dram=out)
                return
            norm_phase(c, "ln1", True)
        elif only == "moe":
            norm_phase(c, "ln1", False)
        if only in (None, "moe"):
            with ExitStack() as moe:
                combine = c.sb(moe, "combine", [P, NT, ALL_EXPERTS], F32)
                router_phase(c, combine, a["gate_w"])
                moe_phase(c, combine, a["wgu"], a["wdn"])
            if only == "moe":
                norm_phase(c, "ln2", True, want_t=False, out_dram=out)
                return
            norm_phase(c, "ln2", True)
        elif only == "gdn":
            norm_phase(c, "ln2", False)
        if only in (None, "gdn"):
            delta_phase(c, a)
            if only == "gdn":
                norm_phase(c, "ln3", True, want_t=False, out_dram=out)
                return
            norm_phase(c, "ln3", True)
        else:
            norm_phase(c, "ln3", False)
        ffn_phase(c, a["ffn_g"], a["ffn_u"], a["ffn_d"], a["ffn_gs"], a["ffn_us"], a["ffn_ds"])
        norm_phase(c, "ln4", True, want_t=False, out_dram=out)


def layout(inputs):
    import numpy as np

    def rows(w, parts):
        return np.ascontiguousarray(w.reshape(parts, P, -1).transpose(1, 0, 2))

    g = {k: np.asarray(v) for k, v in inputs.items()}
    out = {"x": g["L0_attn_x"].reshape(T, D)}
    out["wqkv"] = rows(np.concatenate([g[f"L0_attn_{n}_w"].T for n in "qkv"], 1), KD)
    out["bqkv"] = np.concatenate([g[f"L0_attn_{n}_b"] for n in "qkv"])[None]
    out["out_w"] = rows(g["L0_attn_out_w"].T, KD)
    out["out_b"] = g["L0_attn_out_b"][None]
    inv = (1.0 / np.float32(10000.0) ** (np.arange(0, DH, 2, dtype=np.float32) / np.float32(DH))).astype(np.float32)
    angle = np.arange(T, dtype=np.float32)[:, None] * inv[None]
    cos, sin = np.cos(angle), np.sin(angle)
    table = np.stack([np.concatenate([cos, cos], 1), np.concatenate([-sin, sin], 1)], 1).astype(np.float32)
    out["rope"] = np.ascontiguousarray(table.reshape(NT, P, 2, DH).transpose(1, 0, 2, 3))
    out["gate_w"] = rows(g["L0_ffn_gate_w"].T, KD)
    shared = g["L0_ffn_shared_gate_up"].reshape(D, 2, SHARED_PARTS, INTER).transpose(2, 0, 1, 3)
    wgu = np.concatenate([g["L0_ffn_w_gate_up"], shared.reshape(SHARED_PARTS, D, 2 * INTER)])
    out["wgu"] = np.ascontiguousarray(wgu.reshape(ALL_EXPERTS, KD, P, 2 * INTER).transpose(2, 1, 0, 3))
    pad = np.zeros((HT * P - HCAT, D), np.float32)
    out["wdn"] = rows(np.concatenate([g["L0_ffn_w_down"].reshape(-1, D), g["L0_ffn_shared_down"], pad]), HT)
    kd = HK * DK
    w_qkv, w_z = g["L1_attn_w_qkv"], g["L1_attn_w_z"]
    conv, w_o = g["L1_attn_conv_w"], g["L1_attn_w_out"]
    heads = []
    for h in range(HK):
        cols = [slice(h * DK, (h + 1) * DK), slice(kd + h * DK, kd + (h + 1) * DK)]
        cols += [slice(2 * kd + (VH * h + j) * DK, 2 * kd + (VH * h + j + 1) * DK) for j in range(VH)]
        zcols = slice(VH * h * DK, VH * (h + 1) * DK)
        w = rows(np.concatenate([w_qkv[:, x] for x in cols] + [w_z[:, zcols]], 1), KD).reshape(P, -1)
        taps = np.stack([conv[:, x].T for x in cols], 1).reshape(P, -1)
        heads.append(np.concatenate([w, taps, rows(w_o[zcols], VH).reshape(P, -1)], 1))
    out["w_delta"] = np.stack(heads)
    out["w_ab"] = rows(np.concatenate([g["L1_attn_w_b"], g["L1_attn_w_a"]], 1), KD)
    out["dt_bias"] = g["L1_attn_dt_bias"][None]
    out["a_log"] = g["L1_attn_A_log"][None]
    out["norm_w"] = g["L1_attn_norm_w"][None]
    out["ffn_g"] = rows(g["L1_ffn_gate_w"].T, KD).reshape(P, -1)
    out["ffn_u"] = rows(g["L1_ffn_up_w"].T, KD).reshape(P, -1)
    out["ffn_d"] = rows(g["L1_ffn_down_w"].T, FT).reshape(P, -1)
    out["ffn_gs"] = np.ascontiguousarray(g["L1_ffn_gate_scale"].reshape(FT, P).T)
    out["ffn_us"] = np.ascontiguousarray(g["L1_ffn_up_scale"].reshape(FT, P).T)
    out["ffn_ds"] = g["L1_ffn_down_scale"][None]
    return out


def kernel(**inputs):
    import concourse.bacc as _bacc
    from concourse.bass_utils import run_bass_kernel_spmd as _run

    nc = _bacc.Bacc("TRN2", target_bir_lowering=False, num_devices=1)
    arrays, aps = {}, {}
    for name, arr in layout(inputs).items():
        arrays[f"in_{name}"] = arr
        aps[name] = nc.dram_tensor(f"in_{name}", arr.shape, mybir.dt.from_np(arr.dtype), kind="ExternalInput").ap()
    out = nc.dram_tensor("out_0", (T, D), F32, kind="ExternalOutput").ap()
    program(nc, aps, out)
    r = _run(nc, [arrays], core_ids=[0])
    return r.results[0]["out_0"].reshape(1, T, D)
```
